# Optimizing a Trainium2 kernel written in Bass

```python
import numpy as np
import jax
import jax.numpy as jnp

def _softmax(x, axis=-1):
    return jax.nn.softmax(x, axis=axis)
def _gelu(x):
    return jax.nn.gelu(x, approximate=True)
def _silu(x):
    return jax.nn.silu(x)
def _sigmoid(x):
    return jax.nn.sigmoid(x)
def _layernorm(x, axis=-1, eps=1e-5):
    m = jnp.mean(x, axis=axis, keepdims=True)
    v = jnp.var(x, axis=axis, keepdims=True)
    return (x - m) / jnp.sqrt(v + eps)
def _scatter_add(tgt, idx, src, axis=0):
    return tgt.at[idx].add(src)
def _segment_sum(src, seg, n):
    return jax.ops.segment_sum(src, seg, n)

kernel_name = 'mk_conv_seq_d2_conv_nchw192_914bc8'

def setup_inputs(seed: int = 0):
    np.random.seed(seed)
    _w = jnp.asarray
    def _rec_inputs():
        import jax
        import jax.numpy as jnp
        _gk = jax.random.key(seed)
        x = -0.0001538 + 1 * jax.random.normal(jax.random.fold_in(_gk, 1), (8, 192, 64, 64), jnp.float32)
        return x
    x = _rec_inputs()
    def _L0_conv_setup():
        import jax, jax.numpy as jnp
        import numpy as np
        B, C, H, W = (8, 192, 64, 64)
        D_INNER = 192
        N_STATE = 4
        DT_RANK = 12
        K_DIRS = 4

        def _ln_cf(x, w, b, eps=1e-05):
            mu = x.mean(1, keepdims=True)
            var = ((x - mu) ** 2).mean(1, keepdims=True)
            return (x - mu) / jnp.sqrt(var + eps) * w[None, :, None, None] + b[None, :, None, None]

        def _selective_scan(u, dt, A, Bv, Cv):

            def step(h, inp):
                dt_t, u_t, B_t, C_t = inp
                dA = jnp.exp(dt_t[..., None] * A)
                h = dA * h + dt_t[..., None] * B_t[:, :, None, :] * u_t[..., None]
                y = jnp.einsum('bkdn,bkn->bkd', h, C_t)
                return (h, y)
            h0 = jnp.zeros(u.shape[:3] + (A.shape[-1],), u.dtype)
            xs = (jnp.moveaxis(dt, -1, 0), jnp.moveaxis(u, -1, 0), jnp.moveaxis(Bv, -1, 0), jnp.moveaxis(Cv, -1, 0))
            _, ys = jax.lax.scan(step, h0, xs)
            return jnp.moveaxis(ys, 0, -1)
        key = jax.random.key(seed)
        ks = jax.random.split(key, 8)
        s = 0.02
        return {'x': jax.random.normal(ks[0], (B, C, H, W), jnp.float32), 'ln_w': jnp.ones((C,), jnp.float32), 'ln_b': jnp.zeros((C,), jnp.float32), 'in_proj_w': jax.random.normal(ks[1], (2 * D_INNER, C), jnp.float32) * s, 'conv_w': jax.random.normal(ks[2], (D_INNER, 1, 3, 3), jnp.float32) * s, 'conv_b': jnp.zeros((D_INNER,), jnp.float32), 'x_proj_w': jax.random.normal(ks[3], (K_DIRS, DT_RANK + 2 * N_STATE, D_INNER), jnp.float32) * s, 'dt_proj_w': jax.random.normal(ks[4], (K_DIRS, D_INNER, DT_RANK), jnp.float32) * s, 'dt_proj_b': jnp.full((K_DIRS, D_INNER), -4.6, jnp.float32), 'A_log': jnp.log(jnp.broadcast_to(jnp.arange(1, N_STATE + 1, dtype=jnp.float32), (K_DIRS, D_INNER, N_STATE))), 'Ds': jnp.ones((K_DIRS, D_INNER), jnp.float32), 'out_norm_w': jnp.ones((D_INNER,), jnp.float32), 'out_norm_b': jnp.zeros((D_INNER,), jnp.float32), 'out_proj_w': jax.random.normal(ks[5], (C, D_INNER), jnp.float32) * s}
    _L0_conv_all = _L0_conv_setup()
    _L0_conv_in = {k: v for k, v in _L0_conv_all.items() if k in ('ln_w', 'ln_b', 'in_proj_w', 'conv_w', 'conv_b', 'x_proj_w', 'dt_proj_w', 'dt_proj_b', 'A_log', 'Ds', 'out_norm_w', 'out_norm_b', 'out_proj_w', )}
    del _L0_conv_all

    def _L1_conv_setup():
        import jax, jax.numpy as jnp
        import numpy as np

        def _conv1x1(x, w, b):
            return jnp.einsum('oc,bchw->bohw', w, x) + b[None, :, None, None]
        key = jax.random.key(seed)
        ks = jax.random.split(key, 9)
        B, C, O, H, W = (8, 192, 96, 64, 64)
        s_in = 1.0 / np.sqrt(C)
        s_out = 1.0 / np.sqrt(O)
        return {'x': jax.random.normal(ks[0], (B, C, H, W), dtype=jnp.float32), 'g_w': jax.random.normal(ks[1], (O, C), dtype=jnp.float32) * s_in, 'g_b': jax.random.normal(ks[2], (O,), dtype=jnp.float32) * s_in, 'theta_w': jax.random.normal(ks[3], (O, C), dtype=jnp.float32) * s_in, 'theta_b': jax.random.normal(ks[4], (O,), dtype=jnp.float32) * s_in, 'phi_w': jax.random.normal(ks[5], (O, C), dtype=jnp.float32) * s_in, 'phi_b': jax.random.normal(ks[6], (O,), dtype=jnp.float32) * s_in, 'W_w': jax.random.normal(ks[7], (C, O), dtype=jnp.float32) * s_out, 'W_b': jax.random.normal(ks[8], (C,), dtype=jnp.float32) * s_out}
    _L1_conv_all = _L1_conv_setup()
    _L1_conv_in = {k: v for k, v in _L1_conv_all.items() if k in ('g_w', 'g_b', 'theta_w', 'theta_b', 'phi_w', 'phi_b', 'W_w', 'W_b', )}
    del _L1_conv_all

    return {
        "x": x,
        "L0_conv_ln_w": _L0_conv_in["ln_w"],
        "L0_conv_ln_b": _L0_conv_in["ln_b"],
        "L0_conv_in_proj_w": _L0_conv_in["in_proj_w"],
        "L0_conv_conv_w": _L0_conv_in["conv_w"],
        "L0_conv_conv_b": _L0_conv_in["conv_b"],
        "L0_conv_x_proj_w": _L0_conv_in["x_proj_w"],
        "L0_conv_dt_proj_w": _L0_conv_in["dt_proj_w"],
        "L0_conv_dt_proj_b": _L0_conv_in["dt_proj_b"],
        "L0_conv_A_log": _L0_conv_in["A_log"],
        "L0_conv_Ds": _L0_conv_in["Ds"],
        "L0_conv_out_norm_w": _L0_conv_in["out_norm_w"],
        "L0_conv_out_norm_b": _L0_conv_in["out_norm_b"],
        "L0_conv_out_proj_w": _L0_conv_in["out_proj_w"],
        "L1_conv_g_w": _L1_conv_in["g_w"],
        "L1_conv_g_b": _L1_conv_in["g_b"],
        "L1_conv_theta_w": _L1_conv_in["theta_w"],
        "L1_conv_theta_b": _L1_conv_in["theta_b"],
        "L1_conv_phi_w": _L1_conv_in["phi_w"],
        "L1_conv_phi_b": _L1_conv_in["phi_b"],
        "L1_conv_W_w": _L1_conv_in["W_w"],
        "L1_conv_W_b": _L1_conv_in["W_b"],
    }

def reference(x, L0_conv_ln_w, L0_conv_ln_b, L0_conv_in_proj_w, L0_conv_conv_w, L0_conv_conv_b, L0_conv_x_proj_w, L0_conv_dt_proj_w, L0_conv_dt_proj_b, L0_conv_A_log, L0_conv_Ds, L0_conv_out_norm_w, L0_conv_out_norm_b, L0_conv_out_proj_w, L1_conv_g_w, L1_conv_g_b, L1_conv_theta_w, L1_conv_theta_b, L1_conv_phi_w, L1_conv_phi_b, L1_conv_W_w, L1_conv_W_b):
    import jax
    import jax.numpy as jnp
    def _L0_conv_ref(x, ln_w, ln_b, in_proj_w, conv_w, conv_b, x_proj_w, dt_proj_w, dt_proj_b, A_log, Ds, out_norm_w, out_norm_b, out_proj_w):
        import jax, jax.numpy as jnp
        import numpy as np
        B, C, H, W = (8, 192, 64, 64)
        D_INNER = 192
        N_STATE = 4
        DT_RANK = 12
        K_DIRS = 4

        def _ln_cf(x, w, b, eps=1e-05):
            mu = x.mean(1, keepdims=True)
            var = ((x - mu) ** 2).mean(1, keepdims=True)
            return (x - mu) / jnp.sqrt(var + eps) * w[None, :, None, None] + b[None, :, None, None]

        def _selective_scan(u, dt, A, Bv, Cv):

            def step(h, inp):
                dt_t, u_t, B_t, C_t = inp
                dA = jnp.exp(dt_t[..., None] * A)
                h = dA * h + dt_t[..., None] * B_t[:, :, None, :] * u_t[..., None]
                y = jnp.einsum('bkdn,bkn->bkd', h, C_t)
                return (h, y)
            h0 = jnp.zeros(u.shape[:3] + (A.shape[-1],), u.dtype)
            xs = (jnp.moveaxis(dt, -1, 0), jnp.moveaxis(u, -1, 0), jnp.moveaxis(Bv, -1, 0), jnp.moveaxis(Cv, -1, 0))
            _, ys = jax.lax.scan(step, h0, xs)
            return jnp.moveaxis(ys, 0, -1)
        R = dt_proj_w.shape[-1]
        N = A_log.shape[-1]
        xn = _ln_cf(x, ln_w, ln_b)
        xz = jnp.einsum('dc,bchw->bdhw', in_proj_w, xn)
        xc, z = jnp.split(xz, 2, axis=1)
        xc = jax.lax.conv_general_dilated(xc, conv_w, (1, 1), 'SAME', feature_group_count=xc.shape[1])
        xc = jax.nn.silu(xc + conv_b[None, :, None, None])
        Bsz, D, Hh, Ww = xc.shape
        L = Hh * Ww
        x_hw = xc.reshape(Bsz, D, L)
        x_wh = xc.transpose(0, 1, 3, 2).reshape(Bsz, D, L)
        xs = jnp.stack([x_hw, x_wh, x_hw[..., ::-1], x_wh[..., ::-1]], axis=1)
        x_dbl = jnp.einsum('kcd,bkdl->bkcl', x_proj_w, xs)
        dts, Bv, Cv = jnp.split(x_dbl, [R, R + N], axis=2)
        dt = jnp.einsum('kdr,bkrl->bkdl', dt_proj_w, dts) + dt_proj_b[None, :, :, None]
        dt = jax.nn.softplus(dt)
        A = -jnp.exp(A_log)
        ys = _selective_scan(xs, dt, A, Bv, Cv) + Ds[None, :, :, None] * xs
        y = ys[:, 0] + ys[:, 2, :, ::-1] + ys[:, 1].reshape(Bsz, D, Ww, Hh).transpose(0, 1, 3, 2).reshape(Bsz, D, L) + ys[:, 3, :, ::-1].reshape(Bsz, D, Ww, Hh).transpose(0, 1, 3, 2).reshape(Bsz, D, L)
        y = y.reshape(Bsz, D, Hh, Ww)
        y = _ln_cf(y, out_norm_w, out_norm_b)
        y = y * jax.nn.silu(z)
        out = jnp.einsum('cd,bdhw->bchw', out_proj_w, y)
        return x + out

    def _L1_conv_ref(x, g_w, g_b, theta_w, theta_b, phi_w, phi_b, W_w, W_b):
        import jax, jax.numpy as jnp
        import numpy as np

        def _conv1x1(x, w, b):
            return jnp.einsum('oc,bchw->bohw', w, x) + b[None, :, None, None]
        B, C, H, W = x.shape
        O = g_w.shape[0]
        N = H * W
        g_x = _conv1x1(x, g_w, g_b).reshape(B, O, N)
        theta_x = _conv1x1(x, theta_w, theta_b).reshape(B, O, N)
        phi_x = _conv1x1(x, phi_w, phi_b).reshape(B, O, N)
        f1 = jnp.einsum('bon,bom->bnm', theta_x, phi_x)
        f_div_C = jax.nn.softmax(f1, axis=-1)
        y = jnp.einsum('bnm,bom->bon', f_div_C, g_x)
        y = y.reshape(B, O, H, W)
        W_y = _conv1x1(y, W_w, W_b)
        return W_y + x

    def _gn(v, G=32, eps=1e-5):
        B_, C_, H_, W_ = v.shape
        g = v.reshape(B_, G, C_ // G, H_, W_)
        m = jnp.mean(g, axis=(2, 3, 4), keepdims=True)
        s = jnp.var(g, axis=(2, 3, 4), keepdims=True)
        return ((g - m) / jnp.sqrt(s + eps)).reshape(v.shape)

    def _ln_c(v, eps=1e-6):
        m = jnp.mean(v, axis=1, keepdims=True)
        s = jnp.var(v, axis=1, keepdims=True)
        return (v - m) / jnp.sqrt(s + eps)

    def _ln_t(v, eps=1e-5):
        m = jnp.mean(v, axis=-1, keepdims=True)
        s = jnp.var(v, axis=-1, keepdims=True)
        return (v - m) / jnp.sqrt(s + eps)

    def _to_tokens(v):
        B_, C_, H_, W_ = v.shape
        return v.reshape(B_, C_, H_ * W_).transpose(0, 2, 1)
    def _from_tokens(t, like):
        B_, C_, H_, W_ = like.shape
        return t.transpose(0, 2, 1).reshape(B_, C_, H_, W_)

    x = _L0_conv_ref(x, L0_conv_ln_w, L0_conv_ln_b, L0_conv_in_proj_w, L0_conv_conv_w, L0_conv_conv_b, L0_conv_x_proj_w, L0_conv_dt_proj_w, L0_conv_dt_proj_b, L0_conv_A_log, L0_conv_Ds, L0_conv_out_norm_w, L0_conv_out_norm_b, L0_conv_out_proj_w)
    x = _L1_conv_ref(x, L1_conv_g_w, L1_conv_g_b, L1_conv_theta_w, L1_conv_theta_b, L1_conv_phi_w, L1_conv_phi_b, L1_conv_W_w, L1_conv_W_b)
    return x


_drawn_inputs = setup_inputs


def setup_inputs(seed=0):
    import zlib

    import numpy as np

    out = dict(_drawn_inputs(seed))
    spreads = {'L0_conv_ln_w': (1.0, 0.557),
     'L0_conv_ln_b': (0.0, 0.734),
     'L0_conv_conv_b': (0.0, 0.1),
     'L0_conv_dt_proj_b': (-4.599999904632568, 0.6),
     'L0_conv_Ds': (1.0, 0.6),
     'L0_conv_out_norm_w': (1.0, 0.6),
     'L0_conv_out_norm_b': (0.0, 0.588)}
    factors = {'L0_conv_x_proj_w': 64.0,
     'L0_conv_dt_proj_w': 64.0,
     'L0_conv_A_log': 64.0,
     'L1_conv_phi_b': 64.0}
    for name, (base, spread) in spreads.items():
        noise = np.random.default_rng([zlib.crc32(name.encode()), seed]).standard_normal(out[name].shape)
        drawn = base * np.exp(spread * noise) if base else spread * noise
        out[name] = jnp.asarray(drawn.astype(out[name].dtype))
    for name, factor in factors.items():
        out[name] = (out[name] * factor).astype(out[name].dtype)
    return out
```

```python
from contextlib import ExitStack

import numpy as np
import concourse.bass as bass
from concourse import mybir

F32 = mybir.dt.float32
F32R = mybir.dt.float32r
ALU = mybir.AluOpType
ACT = mybir.ActivationFunctionType
AX = mybir.AxisListType

B, C, HH, WW = 8, 192, 64, 64
L = HH * WW
P = 128
R = C - P
NS, RANK, K = 4, 12, 4
O = 96
T = 512
NCH = L // T
RPC = T // WW
NX = RANK + 2 * NS
NT = NS + NS // 2
NP = NT // 2
LO = 32
PW = WW + 2
G = K * NCH
MT = L // P
MP = MT // 2
ALOG_MAX = 85.0

V_LNW, V_LNB, V_CB, V_DS, V_ONW, V_ONB, V_WB = 0, 2, 4, 6, 14, 16, 18
V_A, V_TAP, V_TB, V_PB, NV = 20, 44, 62, 63, 64


def build(nc, nb, x, vec, w_in, w_x, w_dt, sel, fold, ident, w_out, w_att, gb, w_w, out):
    xr = x.rearrange("b c h w -> b c (h w)")
    outr = out.rearrange("b c h w -> b c (h w)")
    ctx = ExitStack()
    with ctx:
        def sb(name, shape, dt=F32, where=ctx):
            return where.enter_context(nc.sbuf_tensor(name, shape, dt))

        def sem(name):
            return ctx.enter_context(nc.semaphore(name))

        pad0 = sb("pad0", [P, PW * PW])
        pad1 = sb("pad1", [P, PW * PW])
        u0 = sb("u0", [P, L])
        u1 = sb("u1", [P, L])
        g0 = sb("g0", [P, L])
        g1 = sb("g1", [R, L])
        vecs = sb("vecs", [P, NV])
        negA = sb("negA", [P, K * NT])
        dsum = sb("dsum", [P, 2])
        ncb = sb("ncb", [P, 2])
        eps = sb("eps", [P, 1])
        win0 = sb("win0", [P, 448])
        win1 = sb("win1", [R, 448])
        wx0 = sb("wx0", [P, K * 64])
        wx1 = sb("wx1", [P, K * 64])
        wdt = sb("wdt", [NX + 1, K * 2 * P])
        selr = sb("selr", [64, 12 * P], F32R)
        foldw = sb("foldw", [P, R])
        eye = sb("eye", [P, P])
        avg = sb("avg", [P, P])
        wo0 = sb("wo0", [P, C])
        wo1 = sb("wo1", [R, C])
        wa0 = sb("wa0", [P, 3 * O])
        wa1 = sb("wa1", [R, 3 * O])
        gbr = sb("gbr", [1, O])
        ww = sb("ww", [O, C])
        ones = sb("ones", [P, P])

        img = lambda t: t[:, 0:L].rearrange("p (h w) -> p h w", w=WW)
        padi = [pad0[:, :].rearrange("p (h w) -> p h w", w=PW), pad1[:, :].rearrange("p (h w) -> p h w", w=PW)]
        U, Y = [u0, u1], [pad0, pad1]

        def chunk(t, c, order, lo=0, hi=P):
            if order == 0:
                return t[lo:hi, bass.ds(c * T, T)].rearrange("p (a b) -> p a b", b=WW)
            return t[lo:hi, 0:L].rearrange("p (h w) -> p w h", w=WW)[:, bass.ds(c * RPC, RPC), :]

        def flat(ap):
            return ap.rearrange("p (a b) -> p a b", b=WW)

        lnx = ExitStack()
        xa = sb("xa", [P, 2, T], where=lnx)
        xb = sb("xb", [R, 2, T], where=lnx)
        da = sb("da", [P, T], where=lnx)
        db = sb("db", [R, T], where=lnx)
        sqa = sb("sqa", [P, T], where=lnx)
        sqb = sb("sqb", [R, T], where=lnx)
        lnv = sb("lnv", [P, T], where=lnx)
        rstd = sb("rstd", [P, T], where=lnx)
        na = sb("na", [P, T], where=lnx)
        nb_ = sb("nb", [R, T], where=lnx)
        oa = sb("oa", [P, T], where=lnx)
        ob = sb("ob", [R, T], where=lnx)
        yt = sb("yt", [R, T], where=lnx)
        sg = sb("sg", [P, 2, T], where=lnx)
        ta = sb("ta", [P, L], where=lnx)
        lnx.close()
        scx = ExitStack()
        xd = sb("xd", [NX + 1, T], where=scx)
        xhl = [sb(f"xhl{i}", [64, T], F32R, where=scx) for i in range(2)]
        za = sb("za", [P, 2, T], where=scx)
        zl = sb("zl", [P, 2, T], where=scx)
        ze = sb("ze", [P, 2, T], where=scx)
        dt = sb("dt", [P, 2, T], where=scx)
        du = sb("du", [P, 2, T], where=scx)
        dA = sb("dA", [P, 2, 2, T], where=scx)
        bs = sb("bs", [P, 2, 2, T], where=scx)
        dbu = sb("dbu", [P, 2, 2, T], where=scx)
        h = sb("h", [P, 2, NT, T], where=scx)
        hc = sb("hc", [P, 2, T], where=scx)
        scx.close()
        atx = ExitStack()
        sb("hold", [P, 17 * T], where=atx)
        phh = sb("phh", [O + 1, L], F32R, where=atx)
        phl = sb("phl", [O + 1, L], F32R, where=atx)
        gt = sb("gt", [P, MT, O + 1], where=atx)
        atx.close()
        aty = ExitStack()
        pt = sb("pt", [P, 2, 2, T], where=aty)
        thf = sb("thf", [O, T], where=aty)
        thn = [sb(f"thn{i}", [O, T], F32R, where=aty) for i in range(2)]
        thc = [sb(f"thc{i}", [O + 1, T], F32R, where=aty) for i in range(2)]
        mx = sb("mx", [P, 4, 4], where=aty)
        nmx = sb("nmx", [P, 4], where=aty)
        rden = sb("rden", [O + 1, T], where=aty)
        yraw = sb("yraw", [O, T], where=aty)
        yn = sb("yn", [O, T], where=aty)
        fa = sb("fa", [P, 2, T], where=aty)
        aty.close()

        ps = ctx.enter_context(nc.psum_tensor("ps", [P, 8, T], F32))

        s_load = sem("s_load")
        stage_done = sem("stage_done")
        mark = sem("mark")
        stages = 5

        def barrier(eng, b, n):
            eng.sem_inc(mark, 1)
            eng.drain().then_inc(stage_done, 1)
            eng.wait_ge(stage_done, b * (5 * stages) + (5 * (n + 1) + 5))
            eng.sem_inc(mark, 1)

        S = {n: sem(n) for n in (
            "consts_set", "x_loaded0", "x_loaded1", "x_free", "mean_ready", "dev_ready", "sq_ready", "var_ready",
            "rstd_ready", "norm_ready", "proj_ready", "pre_copied", "gexp_ready", "gate_ready", "zeroed", "ln_link", "conv_link", "mix_link", "silu_done",
            "conv_ready", "uexp_ready",
            "xdbl_ready", "xd_ready", "xhi_ready", "xlo_ready", "dtpre_ready", "soft_ready", "res_ready", "sp_ready",
            "dt_ready", "du_ready", "dA_ready", "bbc_ready", "bs_ready", "cbc_ready", "dbu_ready", "scan_link",
            "hc_ready", "summed", "y_added", "zero_h",
            "y_copied", "gated_ready", "x1_ready", "phi_ready", "phf_ready", "phh_ready", "phl_ready", "gt_ready", "gt_copied",
            "theta_ready", "thf_ready", "thh_ready", "thl_ready", "top_ready", "top_read", "nmx_ready", "shift_ready", "thc_ready",
            "st_ready", "pt_ready", "pv_ready", "rden_ready", "rb_ready", "yraw_ready", "yn_ready", "wy_ready", "fin_ready",
            "out_stored", "tail_read")}

        block = ctx.enter_context(nc.Block())
        LOADS = [(vecs[:, :], vec), (win0[:, :], w_in[0:P]), (win1[:, :], w_in[P:C]), (wx0[:, :], w_x[0:P]), (wx1[:, :], w_x[P:2 * P]),
                 (wdt[:, :], w_dt), (foldw[:, :], fold), (eye[:, :], ident), (wo0[:, :], w_out[0:P]), (wo1[:, :], w_out[P:C]),
                 (wa0[:, :], w_att[0:P]), (wa1[:, :], w_att[P:C]), (gbr[:, :], gb), (ww[:, :], w_w), (g0[0:64, 0:12 * P], sel)]
        NL = 16 * len(LOADS)

        def run_chunks(eng, b, body):
            def place(k, n):
                return n if k < 2 else NCH - 1 - n
            for k in range(K):
                with eng.Fori(0, NCH // 2 - 1) as cc:
                    for e in range(2):
                        n = cc * 2 + e
                        body(k, place(k, n), e, b * G + n + k * NCH, k, place(k, n + 1), False)
                for n in (NCH - 2, NCH - 1):
                    nk, nn = (k, n + 1) if n + 1 < NCH else (k + 1, 0)
                    body(k, place(k, n), n % 2, b * G + (k * NCH + n), nk, place(nk, nn), nk == K)

        @block.sync
        def _(sp):
            for dst, src in LOADS:
                sp.dma_start(dst, src).then_inc(s_load, 16)
            sp.wait_ge(s_load, NL)
            barrier(sp, 0, -1)
            with sp.Fori(0, nb) as b:
                def loads(n):
                    with sp.Fori(0, NCH // 2) as cc:
                        for q in range(2):
                            i = (b * 2 + n) * NCH + cc * 2 + q
                            sp.wait_ge(S["x_free"], i + 1)
                            sl = bass.ds((cc * 2 + q) * T, T)
                            sp.dma_start(xa[:, q, :], xr[b, 0:P, sl]).then_inc(S[f"x_loaded{q}"], 16)
                            sp.dma_start(xb[:, q, :], xr[b, P:C, sl]).then_inc(S[f"x_loaded{q}"], 16)
                loads(0)
                barrier(sp, b, 0)
                barrier(sp, b, 1)
                barrier(sp, b, 2)
                loads(1)
                barrier(sp, b, 3)
                with sp.Fori(0, NCH) as c:
                    sp.wait_ge(S["fin_ready"], (b * NCH + c) * 2 + 2)
                    sl = bass.ds(c * T, T)
                    sp.dma_start(outr[b, 0:P, sl], fa[:, 0, :]).then_inc(S["out_stored"], 16)
                    sp.dma_start(outr[b, P:C, sl], fa[0:R, 1, :]).then_inc(S["out_stored"], 16)
                sp.wait_ge(S["out_stored"], b * (32 * NCH) + (32 * NCH + 32))
                barrier(sp, b, 4)

        @block.tensor
        def _(pe):
            mm = pe.matmul
            barrier(pe, 0, -1)

            def mean_of(bank, a, r, s):
                mm(ps[:, bank, :], avg[:, :], a, start=True, stop=False)
                mm(ps[:, bank, :], avg[0:R, :], r, start=False, stop=True).then_inc(S[s], 1)

            with pe.Fori(0, nb) as b:
                with pe.Fori(0, NCH // 2) as cc:
                    for q in range(2):
                        i = b * NCH + cc * 2 + q
                        n = (b * 2) * NCH + cc * 2 + q
                        pe.wait_ge(S[f"x_loaded{q}"], (b * 2) * (16 * NCH) + cc * 32 + 32)
                        mean_of(0, xa[:, q, :], xb[:, q, :], "mean_ready")
                        pe.wait_ge(S["sq_ready"], n * 2 + 2)
                        mean_of(1, sqa[:, :], sqb[:, :], "var_ready")
                        pe.wait_ge(S["norm_ready"], i * 2 + 2)
                        pe.wait_ge(S["gate_ready"], i * 2 + 2)
                        pe.wait_ge(S["pre_copied"], i * 2 + 2)
                        for bank, lo, hi in ((2, 0, 128), (3, 128, 256), (4, 256, 384), (5, 384, 448)):
                            mm(ps[0:hi - lo, bank, :], win0[:, lo:hi], na[:, :], start=True, stop=False)
                            mm(ps[0:hi - lo, bank, :], win1[:, lo:hi], nb_[:, :], start=False, stop=True)\
                                .then_inc(S["proj_ready"], 1)
                barrier(pe, b, 0)
                barrier(pe, b, 1)

                def xdbl(k, c, g):
                    pe.wait_ge(S["xlo_ready"], g + 1)
                    order = k % 2
                    mm(flat(ps[0:64, 0, :]), wx0[:, k * 64:k * 64 + 64], chunk(u0, c, order), start=True, stop=False,
                       skip_group_check=True)
                    mm(flat(ps[0:64, 0, :]), wx1[:, k * 64:k * 64 + 64], chunk(u1, c, order), start=False,
                       stop=True, skip_group_check=True).then_inc(S["xdbl_ready"], 1)

                def dtproj(k, g):
                    pe.wait_ge(S["xd_ready"], g + 1)
                    pe.wait_ge(S["dt_ready"], g + 1)
                    for r in range(2):
                        m = mm(ps[:, 6 + r, :], wdt[:, (2 * k + r) * P:(2 * k + r + 1) * P], xd[:, :],
                               start=True, stop=True)
                    m.then_inc(S["dtpre_ready"], 1)

                def spread(what, q, par):
                    base = 0 if what == "B" else NT
                    bank = 2 if what == "B" else 4
                    for e in range(2):
                        j = base + 2 * q + e
                        m = mm(ps[:, bank + e, :], selr[:, j * P:(j + 1) * P], xhl[par][:, :], start=True, stop=True)
                    m.then_inc(S["bbc_ready" if what == "B" else "cbc_ready"], 1)

                def sumstates(q, g, s):
                    pe.wait_ge(S["hc_ready"], s + 2)
                    if q == 0:
                        pe.wait_ge(S["y_added"], g + 1)
                    for e in range(2):
                        if q < 2:
                            m = mm(ps[:, 1, :], eye[:, :], hc[:, e, :], start=(q == 0 and e == 0),
                                   stop=(q == 1 and e == 1))
                        else:
                            m = mm(ps[R:P, 0, :], foldw[:, :], hc[:, e, :], start=(e == 0), stop=(e == 1),
                                   skip_group_check=True)
                    m.then_inc(S["summed"], 1)

                def body(k, c, par, g, nk, ncx, last):
                    for q in range(NP):
                        s = g * NP + q
                        if q == 0 and not last:
                            xdbl(nk, ncx, g + 1)
                        if not (last and q == NP - 1):
                            if q == NP - 1:
                                pe.wait_ge(S["xlo_ready"], g + 3)
                            pe.wait_ge(S["bs_ready"], s + 2)
                            spread("B", (q + 1) % NP, par if q < NP - 1 else 1 - par)
                        pe.wait_ge(S["hc_ready"], s + 2)
                        spread("C", q, par)
                        if q > 0:
                            sumstates(q - 1, g, s)
                        if q == 0 and not last:
                            dtproj(nk, g + 1)
                    sumstates(NP - 1, g, g * NP + NP)

                g_0 = b * G
                xdbl(0, 0, g_0)
                dtproj(0, g_0)
                pe.wait_ge(S["xlo_ready"], g_0 + 2)
                spread("B", 0, 0)
                run_chunks(pe, b, body)
                barrier(pe, b, 2)

                with pe.Fori(0, NCH // 2) as cc:
                    for q in range(2):
                        c = cc * 2 + q
                        i = b * NCH + c
                        n = (b * 2 + 1) * NCH + c
                        pe.wait_ge(S["y_copied"], i + 1)
                        mean_of(0, pad0[:, bass.ds(c * T, T)], yt[:, :], "mean_ready")
                        pe.wait_ge(S["sq_ready"], n * 2 + 2)
                        mean_of(1, sqa[:, :], sqb[:, :], "var_ready")
                        pe.wait_ge(S["gated_ready"], i * 2 + 2)
                        mm(ps[:, 2, :], wo0[:, 0:P], oa[:, :], start=True, stop=False)
                        mm(ps[:, 2, :], wo1[:, 0:P], ob[:, :], start=False, stop=True)
                        mm(ps[0:R, 3, :], wo0[:, P:C], oa[:, :], start=True, stop=False)
                        mm(ps[0:R, 3, :], wo1[:, P:C], ob[:, :], start=False, stop=True).then_inc(S["proj_ready"], 1)
                        pe.wait_ge(S["x1_ready"], i * 2 + 2)
                        pe.wait_ge(S["phl_ready"], i + 1)
                        mm(ps[0:O, 4, :], wa0[:, O:2 * O], na[:, :], start=True, stop=False)
                        mm(ps[0:O, 4, :], wa1[:, O:2 * O], nb_[:, :], start=False, stop=True)\
                            .then_inc(S["phi_ready"], 1)
                        pe.wait_ge(S["gt_copied"], i + 1)
                        for t in range(T // P):
                            dst = ps[:, 5, t * P:t * P + O]
                            mm(dst, na[:, t * P:(t + 1) * P], wa0[:, 2 * O:3 * O], start=True, stop=False)
                            mm(dst, nb_[:, t * P:(t + 1) * P], wa1[:, 2 * O:3 * O], start=False, stop=False)
                            m = mm(dst, ones[0:1, :], gbr[:, :], start=False, stop=True)
                        m.then_inc(S["gt_ready"], 1)
                barrier(pe, b, 3)

                def theta(c, i, first=False):
                    x1b = pad1[0:R, bass.ds(c * T, T)]
                    if not first:
                        pe.wait_ge(S["tail_read"], i)
                    mm(ps[0:O, 7, :], wa0[:, 0:O], pad0[:, bass.ds(c * T, T)], start=True, stop=False)
                    mm(ps[0:O, 7, :], wa1[:, 0:O], x1b, start=False, stop=True).then_inc(S["theta_ready"], 1)

                def top(j, i):
                    t, m = j // 4, j % 4
                    if j == 0:
                        pe.wait_ge(S["thh_ready"], i + 1)
                    pe.wait_ge(S["top_read"], i * MP + (j + 1))
                    for e in range(2):
                        mc = (2 * m + e) * T
                        q = mm(ps[:, 5 + e, :], thn[0][:, t * P:(t + 1) * P], phh[0:O, mc:mc + T],
                               start=True, stop=True)
                    q.then_inc(S["top_ready"], 1)

                def shift(i):
                    pe.wait_ge(S["nmx_ready"], i + 1)
                    for t in range(4):
                        q = mm(ps[O:O + 1, 7, t * P:(t + 1) * P], nmx[:, t:t + 1], eye[:, :], start=True, stop=True)
                    q.then_inc(S["shift_ready"], 1)

                def scores(mp, i):
                    s = i * MP + mp
                    if mp == 0:
                        pe.wait_ge(S["thc_ready"], i + 1)
                    pe.wait_ge(S["pt_ready"], s + 1)
                    for e in range(2):
                        m = 2 * mp + e
                        dst = ps[:, 2 * (mp % 2) + e, :]
                        kk = phh[:, m * P:(m + 1) * P]
                        mm(dst, kk, thc[0][:, :], start=True, stop=False)
                        mm(dst, phl[:, m * P:(m + 1) * P], thc[0][:, :], start=False, stop=False)
                        q = mm(dst, kk, thc[1][:, :], start=False, stop=True)
                    q.then_inc(S["st_ready"], 1)

                def weigh(mp, i):
                    pe.wait_ge(S["pt_ready"], i * MP + mp + 3)
                    if mp == 0:
                        pe.wait_ge(S["yraw_ready"], i * 2 + 2)
                    for e in range(2):
                        m = 2 * mp + e
                        q = mm(ps[0:O + 1, 4, :], gt[:, m, :], pt[:, mp % 2, e, :], start=(m == 0), stop=(m == MT - 1))
                    q.then_inc(S["pv_ready"], 1)

                def tail(i, nxt):
                    pe.wait_ge(S["rden_ready"], i + 1)
                    if nxt:
                        pe.wait_ge(S["thc_ready"], i + 2)
                    mm(ps[0:O, 7, :], ones[O:O + 1, 0:O], rden[O:O + 1, :], start=True, stop=True)\
                        .then_inc(S["rb_ready"], 1)
                    pe.wait_ge(S["yn_ready"], i + 1)
                    mm(ps[:, 7, :], ww[:, 0:P], yn[:, :], start=True, stop=True)
                    mm(ps[0:R, 6, :], ww[:, P:C], yn[:, :], start=True, stop=True).then_inc(S["wy_ready"], 1)

                def attend(c, i, nxt):
                    if nxt is not None:
                        theta(nxt, i + 1)
                    for mp in range(MP):
                        scores(mp, i)
                        if mp > 0:
                            weigh(mp - 1, i)
                        if nxt is not None:
                            top(mp, i + 1)
                    weigh(MP - 1, i)
                    if nxt is not None:
                        shift(i + 1)
                    tail(i, nxt is not None)

                i_0 = b * NCH
                theta(0, i_0, True)
                for j in range(MP):
                    top(j, i_0)
                shift(i_0)
                with pe.Fori(0, NCH - 1) as c:
                    attend(c, i_0 + c, c + 1)
                attend(NCH - 1, i_0 + NCH - 1, None)
                barrier(pe, b, 4)

        @block.scalar
        def _(act):
            A = act.activation
            act.wait_ge(s_load, NL)
            A(selr[:, :], g0[0:64, 0:12 * P], ACT.Copy)
            act.wait_ge(S["consts_set"], 1)
            A(negA[:, :], negA[:, :], ACT.Exp).then_inc(S["consts_set"], 1)
            act.mul(ncb[:, :], vecs[:, V_CB:V_CB + 2], -1.0)
            barrier(act, 0, -1)
            with act.Fori(0, nb) as b:
                def variance(n, first):
                    act.wait_ge(S["dev_ready"], n * 2 + 2)
                    A(sqa[:, :], da[:, :], ACT.Square).then_inc(S["sq_ready"], 1)
                    A(sqb[:, :], db[:, :], ACT.Square).then_inc(S["sq_ready"], 1)
                    act.wait_ge(S["var_ready"], n + 1)
                    A(lnv[:, :], ps[:, 1, :], ACT.Ln, bias=eps[:, :]).then_inc(S["rstd_ready"], 1)
                    act.wait_ge(S["rstd_ready"], n * 2 + 1)
                    A(rstd[:, :], lnv[:, :], ACT.Exp, scale=-0.5).then_inc(S["rstd_ready"], 1)

                with act.Fori(0, NCH) as c:
                    i = b * NCH + c
                    n = (b * 2) * NCH + c
                    variance(n, True)
                    rows = bass.ds(c * RPC + 1, RPC)
                    pj = (b * (5 * NCH)) + c * 4
                    act.wait_ge(S["proj_ready"], pj + 2)
                    for r in range(2):
                        A(padi[r][:, rows, 1:1 + WW], flat(ps[:, 2 + r, :]), ACT.Copy).then_inc(S["pre_copied"], 1)
                    act.wait_ge(S["proj_ready"], pj + 4)
                    act.wait_ge(S["gate_ready"], i * 2 + 2)
                    A(sg[:, 0, :], ps[:, 4, :], ACT.Exp, scale=-1.0).then_inc(S["gexp_ready"], 1)
                    A(sg[0:R, 1, :], ps[0:R, 5, :], ACT.Exp, scale=-1.0).then_inc(S["gexp_ready"], 1)
                barrier(act, b, 0)
                for r in range(2):
                    act.wait_ge(S["conv_ready"], b * 2 + (r + 1))
                    if r == 1:
                        act.wait_ge(S["silu_done"], b * 2 + 1)
                    A(ta[:, :], U[r][:, :], ACT.Exp, scale=-1.0, bias=ncb[:, r:r + 1]).then_inc(S["uexp_ready"], 1)
                barrier(act, b, 1)

                def front_copy(par, g):
                    act.wait_ge(S["xdbl_ready"], g + 1)
                    act.wait_ge(S["dtpre_ready"], g + 1)
                    A(xd[0:NX, :], ps[0:NX, 0, :], ACT.Copy).then_inc(S["xd_ready"], 1)
                    act.wait_ge(S["summed"], g * NP + 1)
                    A(xhl[par][:, :], ps[0:64, 0, :], ACT.Copy).then_inc(S["xhi_ready"], 1)

                def front_soft(g):
                    act.wait_ge(S["dtpre_ready"], g + 2)
                    A(za[:, :, :], ps[:, 6:8, :], ACT.Abs).then_inc(S["soft_ready"], 1)
                    act.wait_ge(S["soft_ready"], g * 3 + 1)
                    A(za[:, :, :], za[:, :, :], ACT.Exp, scale=-1.0).then_inc(S["soft_ready"], 1)
                    act.wait_ge(S["soft_ready"], g * 3 + 2)
                    A(zl[:, :, :], za[:, :, :], ACT.Ln, bias=1.0).then_inc(S["soft_ready"], 1)

                def decay(k, q, s, g, slot):
                    if q == 0:
                        act.wait_ge(S["dt_ready"], g + 2)
                    act.wait_ge(S["hc_ready"], s + 1)
                    for e in range(2):
                        j = 2 * q + e
                        A(dA[:, slot, e, :], dt[:, 0 if j < NS else 1, :], ACT.Exp,
                          scale=negA[:, k * NT + j:k * NT + j + 1]).then_inc(S["dA_ready"], 1)
                    act.wait_ge(S["bbc_ready"], s + 1)
                    act.wait_ge(S["dbu_ready"], s + 1)
                    A(bs[:, slot, :, :], ps[:, 2:4, :], ACT.Copy).then_inc(S["bs_ready"], 1)

                def body(k, c, par, g, nk, ncx, last):
                    for q in range(NP):
                        s = g * NP + q
                        if q == 0 and not last:
                            front_copy(1 - par, g + 1)
                        if not (last and q == NP - 1):
                            decay(k if q < NP - 1 else nk, (q + 1) % NP, s + 1, g + (q == NP - 1),
                                  (par * NP + q + 1) % 2)
                        if q == 0 and not last:
                            front_soft(g + 1)
                g_0 = b * G
                front_copy(0, g_0)
                front_soft(g_0)
                decay(0, 0, g_0 * NP, g_0, 0)
                run_chunks(act, b, body)
                barrier(act, b, 2)

                with act.Fori(0, NCH) as c:
                    i = b * NCH + c
                    n = (b * 2 + 1) * NCH + c
                    A(yt[:, :], pad1[R:P, bass.ds(c * T, T)], ACT.Copy).then_inc(S["y_copied"], 1)
                    variance(n, False)
                    act.wait_ge(S["x1_ready"], i * 2 + 2)
                    A(pad0[:, bass.ds(c * T, T)], na[:, :], ACT.Copy)
                    A(pad1[0:R, bass.ds(c * T, T)], nb_[:, :], ACT.Copy)
                    act.wait_ge(S["phi_ready"], i + 1)
                    A(lnv[0:O, :], ps[0:O, 4, :], ACT.Identity, bias=vecs[0:O, V_PB:V_PB + 1])\
                        .then_inc(S["phf_ready"], 1)
                    act.wait_ge(S["phf_ready"], i + 1)
                    A(phh[0:O, bass.ds(c * T, T)], lnv[0:O, :], ACT.Copy).then_inc(S["phh_ready"], 1)
                    act.wait_ge(S["gt_ready"], i + 1)
                    A(gt[:, bass.ds(c * 4, 4), 0:O], ps[:, 5, :].rearrange("p (t n) -> p t n", n=P)[:, :, 0:O],
                      ACT.Copy).then_inc(S["gt_copied"], 1)
                    act.wait_ge(S["phl_ready"], i + 2)
                barrier(act, b, 3)

                def split_theta(i):
                    act.wait_ge(S["theta_ready"], i + 1)
                    A(thf[:, :], ps[0:O, 7, :], ACT.Identity, bias=vecs[0:O, V_TB:V_TB + 1])\
                        .then_inc(S["thf_ready"], 1)
                    act.wait_ge(S["thf_ready"], i + 1)
                    A(thn[0][:, :], thf[:, :], ACT.Copy).then_inc(S["thh_ready"], 1)

                def take_theta(i):
                    act.wait_ge(S["thl_ready"], i + 1)
                    act.wait_ge(S["shift_ready"], i + 1)
                    A(thc[0][0:O, :], thn[0][:, :].bitcast(F32), ACT.Copy)
                    A(thc[1][0:O, :], thn[1][:, :].bitcast(F32), ACT.Copy)
                    A(thc[0][O:O + 1, :], ps[O:O + 1, 7, :], ACT.Copy).then_inc(S["thc_ready"], 1)

                def attend(c, i, nxt):
                    if nxt:
                        split_theta(i + 1)
                    for mp in range(MP):
                        s = i * MP + mp
                        act.wait_ge(S["st_ready"], s + 1)
                        act.wait_ge(S["pv_ready"], s + 1)
                        A(pt[:, mp % 2, :, :], ps[:, 2 * (mp % 2):2 * (mp % 2) + 2, :], ACT.Exp)\
                            .then_inc(S["pt_ready"], 1)
                    if nxt:
                        take_theta(i + 1)
                    act.wait_ge(S["pv_ready"], i * MP + MP + 2)
                    A(yraw[:, :], ps[0:O, 4, :], ACT.Copy).then_inc(S["yraw_ready"], 1)
                i_0 = b * NCH
                split_theta(i_0)
                take_theta(i_0)
                with act.Fori(0, NCH - 1) as c:
                    attend(c, i_0 + c, True)
                attend(NCH - 1, i_0 + NCH - 1, False)
                barrier(act, b, 4)

        @block.gpsimd
        def _(pool):
            pool.wait_ge(s_load, NL)
            pool.memset(avg[:, :], 1.0 / C)
            pool.memset(ones[:, :], 1.0)
            pool.memset(eps[:, :], 1e-5)
            barrier(pool, 0, -1)
            with pool.Fori(0, nb) as b:
                barrier(pool, b, 0)
                barrier(pool, b, 1)

                def residue(g):
                    pool.wait_ge(S["res_ready"], g * 2 + 2)
                    pool.wait_ge(S["soft_ready"], g * 3 + 3)
                    pool.tensor_tensor(zl[:, :, :], zl[:, :, :], ze[:, :, :], ALU.add).then_inc(S["sp_ready"], 1)

                def times_u(k, c, g):
                    pool.wait_ge(S["dt_ready"], g + 2)
                    pool.wait_ge(S["dbu_ready"], g * NP + 2)
                    for r in range(2):
                        m = pool.tensor_tensor(flat(du[:, r, :]), flat(dt[:, r, :]), chunk(U[r], c, k % 2), ALU.mult)
                        m.then_inc(S["du_ready"], 1)
                    pool.wait_ge(S["du_ready"], g * 2 + 2)

                def drive(q, s, slot):
                    pool.wait_ge(S["bs_ready"], s + 2)
                    pool.wait_ge(S["hc_ready"], s + 1)
                    r = 0 if 2 * q < NS else 1
                    pool.tensor_tensor(dbu[:, slot, :, :], bs[:, slot, :, :],
                                       du[:, r:r + 1, :].to_broadcast([P, 2, T]), ALU.mult).then_inc(S["dbu_ready"], 1)

                def body(k, c, par, g, nk, ncx, last):
                    for q in range(NP):
                        s = g * NP + q
                        if q == NP - 1 and not last:
                            times_u(nk, ncx, g + 1)
                        if not (last and q == NP - 1):
                            drive((q + 1) % NP, s + 1, (par * NP + q + 1) % 2)
                        if q == 0 and not last:
                            residue(g + 1)
                g_0 = b * G
                residue(g_0)
                times_u(0, 0, g_0)
                drive(0, g_0 * NP, 0)
                run_chunks(pool, b, body)
                barrier(pool, b, 2)
                barrier(pool, b, 3)
                barrier(pool, b, 4)

        @block.vector
        def _(dve):
            TT, TS, STT = dve.tensor_tensor, dve.tensor_scalar, dve.scalar_tensor_tensor
            dve.wait_ge(s_load, NL)
            TS(negA[:, :], vecs[:, V_A:V_A + K * NT], ALOG_MAX, None, ALU.min).then_inc(S["consts_set"], 1)
            for r in range(2):
                dve.tensor_reduce(dsum[:, r:r + 1], vecs[:, V_DS + 4 * r:V_DS + 4 * r + 4], AX.X, ALU.add)
            dve.wait_ge(S["consts_set"], 2)
            TS(negA[:, :], negA[:, :], -1.0, None, ALU.mult)
            for name, n in (("x_free", 2), ("gate_ready", 2), ("pre_copied", 2), ("xlo_ready", 1), ("dt_ready", 1),
                            ("hc_ready", 2), ("summed", 4), ("y_added", 1), ("bs_ready", 1), ("dbu_ready", 2),
                            ("dtpre_ready", 1), ("phl_ready", 1), ("gt_copied", 1), ("tail_read", 1), ("top_read", 1),
                            ("pt_ready", 2), ("yraw_ready", 2), ("pv_ready", 2), ("out_stored", 32)):
                dve.sem_inc(S[name], n)
            barrier(dve, 0, -1)

            def link(ins, name, n):
                ins.then_inc(S[name], 1)
                dve.wait_ge(S[name], n)

            with dve.Fori(0, nb) as b:
                for t in (pad0, pad1):
                    dve.memset(t[:, :], 0.0)
                dve.memset(sg[:, 1, :], 0.0)
                with dve.Fori(0, NCH // 2) as cc:
                    for q in range(2):
                        c = cc * 2 + q
                        i = b * NCH + c
                        n = (b * 2) * NCH + c
                        dve.wait_ge(S["mean_ready"], n + 1)
                        TT(da[:, :], xa[:, q, :], ps[:, 0, :], ALU.subtract).then_inc(S["dev_ready"], 1)
                        TT(db[:, :], xb[:, q, :], ps[0:R, 0, :], ALU.subtract).then_inc(S["dev_ready"], 1)
                        dve.wait_ge(S["dev_ready"], n * 2 + 2)
                        dve.sem_inc(S["x_free"], 1)
                        dve.wait_ge(S["rstd_ready"], n * 2 + 2)
                        at = i * 4
                        link(TT(da[:, :], da[:, :], rstd[:, :], ALU.mult), "ln_link", at + 1)
                        link(TT(db[:, :], db[:, :], rstd[0:R, :], ALU.mult), "ln_link", at + 2)
                        TS(na[:, :], da[:, :], vecs[:, V_LNW:V_LNW + 1], vecs[:, V_LNB:V_LNB + 1], ALU.mult, ALU.add)\
                            .then_inc(S["norm_ready"], 1)
                        TS(nb_[:, :], db[:, :], vecs[0:R, V_LNW + 1:V_LNW + 2], vecs[0:R, V_LNB + 1:V_LNB + 2],
                           ALU.mult, ALU.add).then_inc(S["norm_ready"], 1)
                        dve.wait_ge(S["gexp_ready"], i * 2 + 2)
                        link(TS(sg[:, :, :], sg[:, :, :], 1.0, None, ALU.add), "ln_link", at + 3)
                        link(dve.reciprocal(sg[:, :, :], sg[:, :, :]), "ln_link", at + 4)
                        sl = bass.ds(c * T, T)
                        TT(g0[:, sl], ps[:, 4, :], sg[:, 0, :], ALU.mult).then_inc(S["gate_ready"], 1)
                        TT(g1[:, sl], ps[0:R, 5, :], sg[0:R, 1, :], ALU.mult).then_inc(S["gate_ready"], 1)
                barrier(dve, b, 0)

                at = b * 21
                n = 0
                for r in range(2):
                    acc = img(U[r])
                    for t in range(9):
                        dy, dx = t // 3, t % 3
                        src = padi[r][:, dy:dy + HH, dx:dx + WW]
                        w = vecs[:, V_TAP + 9 * r + t:V_TAP + 9 * r + t + 1]
                        ins = TS(acc, src, w, None, ALU.mult) if t == 0 else STT(acc, src, w, acc, ALU.mult, ALU.add)
                        if t < 8:
                            n += 1
                            link(ins, "conv_link", at + n)
                    ins.then_inc(S["conv_ready"], 1)
                    dve.wait_ge(S["uexp_ready"], b * 2 + (r + 1))
                    link(TS(ta[:, :], ta[:, :], 1.0, None, ALU.add), "conv_link", at + (n + 1))
                    link(dve.reciprocal(ta[:, :], ta[:, :]), "conv_link", at + (n + 2))
                    n += 2
                    STT(U[r][:, :], U[r][:, :], vecs[:, V_CB + r:V_CB + r + 1], ta[:, :], ALU.add, ALU.mult)\
                        .then_inc(S["silu_done"], 1)
                    dve.wait_ge(S["silu_done"], b * 2 + (r + 1))
                    lo = 0 if r == 0 else R
                    TS(Y[r][lo:P, 0:L], U[r][lo:P, :], dsum[lo:P, r:r + 1], None, ALU.mult)
                dve.memset(xd[:, :], 1.0)
                link(dve.memset(h[:, 1, :, T - 1:T], 0.0), "conv_link", at + (n + 1))
                assert n + 1 == 21
                barrier(dve, b, 1)

                def low_half(par, g):
                    dve.wait_ge(S["xhi_ready"], g + 1)
                    TT(xhl[par][LO:LO + 32, :], ps[LO:LO + 32, 0, :], xhl[par][LO:LO + 32, :].bitcast(F32),
                       ALU.subtract).then_inc(S["xlo_ready"], 1)

                def residue(g):
                    dve.wait_ge(S["soft_ready"], g * 3 + 2)
                    TS(ze[:, :, :], za[:, :, :], 1.0, -1.0, ALU.add, ALU.add).then_inc(S["res_ready"], 1)
                    dve.wait_ge(S["res_ready"], g * 2 + 1)
                    TT(ze[:, :, :], za[:, :, :], ze[:, :, :], ALU.subtract).then_inc(S["res_ready"], 1)

                def softplus(g):
                    dve.wait_ge(S["sp_ready"], g + 1)
                    STT(dt[:, :, :], ps[:, 6:8, :], 0.0, zl[:, :, :], ALU.max, ALU.add).then_inc(S["dt_ready"], 1)

                def scans(k, par, q, s, slot):
                    step = -1 if k >= 2 else 1
                    end = T - 1 if step == 1 else 0
                    dve.wait_ge(S["dA_ready"], s * 2 + 2)
                    dve.wait_ge(S["dbu_ready"], s + 3)
                    for e in range(2):
                        j = 2 * q + e
                        dve.tensor_tensor_scan(h[:, par, j, ::step], dA[:, slot, e, ::step], dbu[:, slot, e, ::step],
                                               h[:, 1 - par, j, end:end + 1], ALU.mult, ALU.add)\
                            .then_inc(S["scan_link"], 1)

                def times_c(par, q, s):
                    dve.wait_ge(S["scan_link"], s * 2 + 2)
                    dve.wait_ge(S["cbc_ready"], s + 1)
                    dve.wait_ge(S["summed"], s + 4)
                    TT(hc[:, :, :], h[:, par, 2 * q:2 * q + 2, :], ps[:, 4:6, :], ALU.mult).then_inc(S["hc_ready"], 1)

                def add_y(k, c, g):
                    dve.wait_ge(S["summed"], g * NP + (NP + 4))
                    if isinstance(c, int) or k >= 2:
                        dve.sem_inc(mark, 1)
                    for r, (lo, bank) in enumerate(((0, 1), (R, 0))):
                        y = chunk(Y[r], c, k % 2, lo, P)
                        ins = TT(y, flat(ps[lo:P, bank, :]), y, ALU.add)
                    ins.then_inc(S["y_added"], 1)

                def body(k, c, par, g, nk, ncx, last):
                    for q in range(NP):
                        s = g * NP + q
                        scans(k, par, q, s, (par * NP + q) % 2)
                        times_c(par, q, s)
                        if q == 0 and not last:
                            low_half(1 - par, g + 1)
                            residue(g + 1)
                        if q == 1 and not last:
                            dve.wait_ge(S["dA_ready"], g * NT + NT)
                            dve.wait_ge(S["du_ready"], g * 2 + 2)
                            softplus(g + 1)
                    add_y(k, c, g)
                    if nk != k and not last:
                        end = T - 1 if nk < 2 else 0
                        dve.memset(h[:, par, :, end:end + 1], 0.0).then_inc(S["zero_h"], 1)
                        dve.wait_ge(S["zero_h"], b * (K - 1) + (k + 1))
                        dve.sem_inc(mark, 1)
                g_0 = b * G
                low_half(0, g_0)
                residue(g_0)
                softplus(g_0)
                run_chunks(dve, b, body)
                barrier(dve, b, 2)

                dve.memset(gt[:, :, O:O + 1], 1.0)
                dve.memset(phh[O:O + 1, :].bitcast(F32), 1.0)
                dve.memset(phl[O:O + 1, :].bitcast(F32), 0.0)
                with dve.Fori(0, NCH // 2) as cc:
                    for q in range(2):
                        c = cc * 2 + q
                        i = b * NCH + c
                        n = (b * 2 + 1) * NCH + c
                        sl = bass.ds(c * T, T)
                        dve.wait_ge(S["mean_ready"], n + 1)
                        TT(da[:, :], pad0[:, sl], ps[:, 0, :], ALU.subtract).then_inc(S["dev_ready"], 1)
                        TT(db[:, :], yt[:, :], ps[0:R, 0, :], ALU.subtract).then_inc(S["dev_ready"], 1)
                        dve.wait_ge(S["rstd_ready"], n * 2 + 2)
                        at = i * 4
                        link(TT(da[:, :], da[:, :], rstd[:, :], ALU.mult), "mix_link", at + 1)
                        link(TT(db[:, :], db[:, :], rstd[0:R, :], ALU.mult), "mix_link", at + 2)
                        link(TS(da[:, :], da[:, :], vecs[:, V_ONW:V_ONW + 1], vecs[:, V_ONB:V_ONB + 1],
                                ALU.mult, ALU.add), "mix_link", at + 3)
                        link(TS(db[:, :], db[:, :], vecs[0:R, V_ONW + 1:V_ONW + 2], vecs[0:R, V_ONB + 1:V_ONB + 2],
                                ALU.mult, ALU.add), "mix_link", at + 4)
                        TT(oa[:, :], da[:, :], g0[:, sl], ALU.mult).then_inc(S["gated_ready"], 1)
                        TT(ob[:, :], db[:, :], g1[:, sl], ALU.mult).then_inc(S["gated_ready"], 1)
                        dve.wait_ge(S["proj_ready"], b * (5 * NCH) + c + (4 * NCH + 1))
                        dve.wait_ge(S[f"x_loaded{q}"], (b * 2 + 1) * (16 * NCH) + cc * 32 + 32)
                        TT(na[:, :], ps[:, 2, :], xa[:, q, :], ALU.add).then_inc(S["x1_ready"], 1)
                        TT(nb_[:, :], ps[0:R, 3, :], xb[:, q, :], ALU.add).then_inc(S["x1_ready"], 1)
                        dve.wait_ge(S["x1_ready"], i * 2 + 2)
                        dve.sem_inc(S["x_free"], 1)
                        dve.wait_ge(S["phh_ready"], i + 1)
                        TT(phl[0:O, sl], lnv[0:O, :], phh[0:O, sl].bitcast(F32), ALU.subtract)\
                            .then_inc(S["phl_ready"], 1)
                        dve.wait_ge(S["gt_ready"], i + 1)
                barrier(dve, b, 3)

                def low_theta(i):
                    dve.wait_ge(S["thh_ready"], i + 1)
                    TT(thn[1][:, :], thf[:, :], thn[0][:, :].bitcast(F32), ALU.subtract).then_inc(S["thl_ready"], 1)

                def top(j, i):
                    dve.wait_ge(S["top_ready"], i * MP + (j + 1))
                    dve.tensor_reduce(mx[:, j // 4, j % 4:j % 4 + 1], ps[:, 5:7, :], AX.XY, ALU.max)\
                        .then_inc(S["top_read"], 1)

                def negate(i, first=False):
                    dve.wait_ge(S["top_read"], i * MP + MP + 1)
                    if not first:
                        dve.wait_ge(S["shift_ready"], i)
                    dve.tensor_reduce(nmx[:, :], mx[:, :, :], AX.X, ALU.max, negate=True).then_inc(S["nmx_ready"], 1)

                def tail(c, i):
                    dve.wait_ge(S["pv_ready"], i * MP + (MP + 2))
                    dve.reciprocal(rden[O:O + 1, :], ps[O:O + 1, 4, :]).then_inc(S["rden_ready"], 1)
                    dve.wait_ge(S["rden_ready"], i + 1)
                    dve.sem_inc(S["yraw_ready"], 1)
                    dve.wait_ge(S["yraw_ready"], i * 2 + 4)
                    dve.wait_ge(S["rb_ready"], i + 1)
                    TT(yn[:, :], yraw[:, :], ps[0:O, 7, :], ALU.mult).then_inc(S["yn_ready"], 1)
                    dve.wait_ge(S["wy_ready"], i + 1)
                    sl = bass.ds(c * T, T)
                    dve.wait_ge(S["out_stored"], i * 32 + 32)
                    STT(fa[:, 0, :], ps[:, 7, :], vecs[:, V_WB:V_WB + 1], pad0[:, sl], ALU.add, ALU.add)\
                        .then_inc(S["fin_ready"], 1)
                    STT(fa[0:R, 1, :], ps[0:R, 6, :], vecs[0:R, V_WB + 1:V_WB + 2], pad1[0:R, sl], ALU.add, ALU.add)\
                        .then_inc(S["fin_ready"], 1)
                    dve.wait_ge(S["fin_ready"], i * 2 + 2)
                    dve.sem_inc(S["tail_read"], 1)

                def attend(c, i, nxt):
                    if nxt:
                        low_theta(i + 1)
                        for j in range(MP):
                            top(j, i + 1)
                        negate(i + 1)
                    tail(c, i)
                i_0 = b * NCH
                dve.memset(thc[1][O:O + 1, :].bitcast(F32), 0.0)
                low_theta(i_0)
                for j in range(MP):
                    top(j, i_0)
                negate(i_0, True)
                with dve.Fori(0, NCH - 1) as c:
                    attend(c, i_0 + c, True)
                attend(NCH - 1, i_0 + NCH - 1, False)
                barrier(dve, b, 4)


def kernel(x, L0_conv_ln_w, L0_conv_ln_b, L0_conv_in_proj_w, L0_conv_conv_w, L0_conv_conv_b, L0_conv_x_proj_w,
           L0_conv_dt_proj_w, L0_conv_dt_proj_b, L0_conv_A_log, L0_conv_Ds, L0_conv_out_norm_w, L0_conv_out_norm_b,
           L0_conv_out_proj_w, L1_conv_g_w, L1_conv_g_b, L1_conv_theta_w, L1_conv_theta_b, L1_conv_phi_w,
           L1_conv_phi_b, L1_conv_W_w, L1_conv_W_b, _nb=B, _run=None):
    f = lambda a: np.ascontiguousarray(np.asarray(a))
    rem2 = lambda a: np.concatenate([a[..., P:C], a[..., P:C]], -1)

    vec = np.zeros((P, NV), np.float32)

    def put(col, v, twice=False):
        v = f(v)
        vec[:, col] = v[:P]
        vec[:, col + 1] = rem2(v)
    for col, v in ((V_LNW, L0_conv_ln_w), (V_LNB, L0_conv_ln_b), (V_CB, L0_conv_conv_b), (V_ONW, L0_conv_out_norm_w),
                   (V_ONB, L0_conv_out_norm_b), (V_WB, L1_conv_W_b)):
        put(col, v)
    ds, al, cw = f(L0_conv_Ds), f(L0_conv_A_log), f(L0_conv_conv_w).reshape(C, 9)
    for k in range(K):
        vec[:, V_DS + k], vec[:, V_DS + 4 + k] = ds[k, :P], rem2(ds[k])
        for n in range(NS):
            vec[:, V_A + k * NT + n] = al[k, :P, n]
        for m in range(NS // 2):
            vec[:, V_A + k * NT + NS + m] = np.concatenate([al[k, P:, 2 * m], al[k, P:, 2 * m + 1]])
    for t in range(9):
        vec[:, V_TAP + t], vec[:, V_TAP + 9 + t] = cw[:P, t], rem2(cw[:, t])
    vec[:O, V_TB], vec[:O, V_PB] = f(L1_conv_theta_b), f(L1_conv_phi_b)

    wi = f(L0_conv_in_proj_w).T
    w_in = np.concatenate([wi[:, :P], rem2(wi[:, :C]), wi[:, C:C + P], wi[:, C + P:]], 1)
    xp, dp, db = f(L0_conv_x_proj_w), f(L0_conv_dt_proj_w), f(L0_conv_dt_proj_b)
    w_x = np.zeros((2 * P, K * 64), np.float32)
    w_dt = np.zeros((NX + 1, K * 2 * P), np.float32)
    for k in range(K):
        w_x[:C, 64 * k:64 * k + NX] = w_x[:C, 64 * k + LO:64 * k + LO + NX] = xp[k].T
        both = np.concatenate([dp[k].T, np.zeros((2 * NS, C), np.float32), db[k][None]], 0)
        w_dt[:, 2 * k * P:(2 * k + 1) * P], w_dt[:, (2 * k + 1) * P:(2 * k + 2) * P] = both[:, :P], rem2(both)
    sel = np.zeros((64, 2 * NT, P), np.float32)
    for w in range(2):
        for j in range(NT):
            for p in range(P):
                n = j if j < NS else 2 * (j - NS) + p // R
                sel[RANK + w * NS + n, w * NT + j, p] = sel[LO + RANK + w * NS + n, w * NT + j, p] = 1.0
    arrays = {
        "x": f(x)[:_nb], "vec": vec, "w_in": w_in, "w_x": w_x, "w_dt": w_dt, "sel": sel.reshape(64, 2 * NT * P),
        "fold": np.concatenate([np.eye(R, dtype=np.float32)] * 2, 0), "ident": np.eye(P, dtype=np.float32),
        "w_out": f(L0_conv_out_proj_w).T,
        "w_att": np.concatenate([f(L1_conv_theta_w).T, f(L1_conv_phi_w).T, f(L1_conv_g_w).T], 1),
        "gb": f(L1_conv_g_b)[None], "w_w": f(L1_conv_W_w).T,
    }
    arrays = {f"in_{n}": np.ascontiguousarray(a) for n, a in arrays.items()}
    import concourse.bacc as bacc
    from concourse.bass_utils import run_bass_kernel_spmd
    nc = bacc.Bacc("TRN2", target_bir_lowering=False, num_devices=1)
    aps = [nc.dram_tensor(n, a.shape, F32, kind="ExternalInput").ap() for n, a in arrays.items()]
    res = nc.dram_tensor("out", [_nb, C, HH, WW], F32, kind="ExternalOutput").ap()
    build(nc, _nb, *aps, res)
    if _run:
        return _run(nc, arrays)
    return run_bass_kernel_spmd(nc, [arrays], core_ids=[0]).results[0]["out"]
```

```python
from contextlib import ExitStack

import numpy as np
import concourse.bass as bass
from concourse import mybir

F32 = mybir.dt.float32
F32R = mybir.dt.float32r
ALU = mybir.AluOpType
ACT = mybir.ActivationFunctionType
AX = mybir.AxisListType

B, C, HH, WW = 8, 192, 64, 64
L = HH * WW
P = 128
R = C - P
NS, RANK, K = 4, 12, 4
O = 96
T = 512
NCH = L // T
RPC = T // WW
NX = RANK + 2 * NS
NT = NS + NS // 2
NP = NT // 2
LO = 32
PW = WW + 2
G = K * NCH
MT = L // P
MP = MT // 2
ALOG_MAX = 85.0

V_LNW, V_LNB, V_CB, V_DS, V_ONW, V_ONB, V_WB = 0, 2, 4, 6, 14, 16, 18
V_A, V_TAP, V_TB, V_PB, NV = 20, 44, 62, 63, 64


def build(nc, nb, x, vec, w_in, w_x, w_dt, sel, fold, ident, w_out, w_att, gb, w_w, out):
    xr = x.rearrange("b c h w -> b c (h w)")
    outr = out.rearrange("b c h w -> b c (h w)")
    ctx = ExitStack()
    with ctx:
        def sb(name, shape, dt=F32, where=ctx):
            return where.enter_context(nc.sbuf_tensor(name, shape, dt))

        def sem(name):
            return ctx.enter_context(nc.semaphore(name))

        pad0 = sb("pad0", [P, PW * PW])
        pad1 = sb("pad1", [P, PW * PW])
        gate = sb("gate", [P, 2, L])
        ux = ExitStack()
        u = sb("u", [P, 2, L], where=ux)
        ux.close()
        kx = ExitStack()
        phh = sb("phh", [O + 1, L], F32R, where=kx)
        phl = sb("phl", [O + 1, L], F32R, where=kx)
        ctx.push(kx)
        vecs = sb("vecs", [P, NV])
        negA = sb("negA", [P, K * NT])
        dsum = sb("dsum", [P, 2])
        eps = sb("eps", [P, 1])
        win0 = sb("win0", [P, 4 * P])
        win1 = sb("win1", [R, 4 * P])
        wx0 = sb("wx0", [P, K * 64])
        wx1 = sb("wx1", [P, K * 64])
        wdt = sb("wdt", [NX + 1, K * 2 * P])
        selr = sb("selr", [64, 12 * P], F32R)
        foldw = sb("foldw", [P, R])
        eye = sb("eye", [P, P])
        avg = sb("avg", [P, P])
        wo0 = sb("wo0", [P, C])
        wo1 = sb("wo1", [R, C])
        wa0 = sb("wa0", [P, 3 * O])
        wa1 = sb("wa1", [R, 3 * O])
        gbr = sb("gbr", [1, O])
        ww = sb("ww", [O, C])
        ones = sb("ones", [P, P])

        padi = [pad0[:, :].rearrange("p (h w) -> p h w", w=PW), pad1[:, :].rearrange("p (h w) -> p h w", w=PW)]
        Y = [pad0, pad1]

        def chunk(t, c, order, lo=0, hi=P):
            if order == 0:
                return t[lo:hi, bass.ds(c * T, T)].rearrange("p (a b) -> p a b", b=WW)
            return t[lo:hi, 0:L].rearrange("p (h w) -> p w h", w=WW)[:, bass.ds(c * RPC, RPC), :]

        def flat(ap):
            return ap.rearrange("p (a b) -> p a b", b=WW)

        vx = ExitStack()
        gth = sb("gth", [P, MT, O + 1], F32R, where=vx)
        gtl = sb("gtl", [P, MT, O + 1], F32R, where=vx)
        lnx = ExitStack()
        xa = sb("xa", [P, 2, T], where=lnx)
        xb = sb("xb", [R, 2, T], where=lnx)
        da = sb("da", [P, T], where=lnx)
        db = sb("db", [R, T], where=lnx)
        sqa = sb("sqa", [P, T], where=lnx)
        sqb = sb("sqb", [R, T], where=lnx)
        lnv = sb("lnv", [P, T], where=lnx)
        rstd = sb("rstd", [P, T], where=lnx)
        na = sb("na", [P, T], where=lnx)
        nb_ = sb("nb", [R, T], where=lnx)
        oa = sb("oa", [P, T], where=lnx)
        ob = sb("ob", [R, T], where=lnx)
        yt = sb("yt", [R, 2, T], where=lnx)
        phf = sb("phf", [O, T], where=lnx)
        zs = sb("zs", [P, 2, T], where=lnx)
        cs = sb("cs", [P, 2, T], where=lnx)
        lnx.close()
        aty = ExitStack()
        pf = sb("pf", [P, 2, 2, T], where=aty)
        ph = sb("ph", [P, 2, 2, T], F32R, where=aty)
        pl = sb("pl", [P, 2, 2, T], F32R, where=aty)
        thf = sb("thf", [O, T], where=aty)
        thn = [sb(f"thn{i}", [O, T], F32R, where=aty) for i in range(2)]
        thc = [[sb(f"thc{q}{i}", [O + 1, T], F32R, where=aty) for i in range(2)] for q in range(2)]
        mx = sb("mx", [P, 4, 4], where=aty)
        nmx = sb("nmx", [P, 4], where=aty)
        rden = sb("rden", [O + 1, T], where=aty)
        yraw = sb("yraw", [O + 1, T], where=aty)
        yn = sb("yn", [O, T], where=aty)
        fa = sb("fa", [P, 2, T], where=aty)
        aty.close()
        vx.close()
        scx = ExitStack()
        xd = sb("xd", [NX + 1, T], where=scx)
        xhl = [sb(f"xhl{i}", [64, T], F32R, where=scx) for i in range(2)]
        za = sb("za", [P, 2, T], where=scx)
        zl = sb("zl", [P, 2, T], where=scx)
        ze = sb("ze", [P, 2, T], where=scx)
        dt = sb("dt", [P, 2, T], where=scx)
        du = sb("du", [P, 2, T], where=scx)
        dA = sb("dA", [P, 2, 2, T], where=scx)
        bs = sb("bs", [P, 2, 2, T], where=scx)
        dbu = sb("dbu", [P, 2, 2, T], where=scx)
        h = sb("h", [P, 2, NT, T], where=scx)
        hc = sb("hc", [P, 2, T], where=scx)
        scx.close()

        ps = ctx.enter_context(nc.psum_tensor("ps", [P, 8, T], F32))

        s_load = sem("s_load")
        stage_done = sem("stage_done")
        mark = sem("mark")
        stages = 4

        def barrier(eng, b, n):
            eng.sem_inc(mark, 1)
            eng.drain().then_inc(stage_done, 1)
            eng.wait_ge(stage_done, b * (5 * stages) + (5 * (n + 1) + 5))
            eng.sem_inc(mark, 1)

        S = {n: sem(n) for n in (
            "consts_set", "borders_set", "scan_set", "att_set", "thc_set",
            "x_loaded0", "x_loaded1", "x_free", "mean_ready", "dev_ready", "sq_ready", "var_ready", "rstd_ready",
            "scaled", "norm_ready", "z_ready", "xc_ready", "zs_ready", "gate_ready", "pre_copied", "tap_ready",
            "conv_link", "conv_ready", "cs_ready", "u_ready",
            "xdbl_ready", "xd_ready", "xhi_ready", "xlo_ready", "dtpre_ready", "soft_ready", "res_ready", "sp_ready",
            "dt_ready", "du_ready", "dA_ready", "bbc_ready", "bs_ready", "cbc_ready", "dbu_ready", "scan_link",
            "hc_ready", "summed", "y_added", "zero_h",
            "yt_ready", "mix_link", "gated_ready", "mixed", "x1_ready", "phi_ready", "phf_ready", "phh_ready", "phl_ready",
            "gt_ready", "gth_ready", "gtl_ready",
            "theta_ready", "thf_ready", "thh_ready", "thl_ready", "top_ready", "top_read", "nmx_ready", "shift_ready",
            "thc_ready", "st_ready", "pf_ready", "ph_ready", "pl_ready", "pv_ready", "yraw_ready", "rden_ready",
            "rb_ready", "yn_ready", "wy_ready", "fin_ready", "out_stored")}

        block = ctx.enter_context(nc.Block())
        LOADS = [(vecs[:, :], vec), (win0[:, :], w_in[0:P]), (win1[:, :], w_in[P:C]), (wx0[:, :], w_x[0:P]), (wx1[:, :], w_x[P:2 * P]),
                 (wdt[:, :], w_dt), (foldw[:, :], fold), (eye[:, :], ident), (wo0[:, :], w_out[0:P]), (wo1[:, :], w_out[P:C]),
                 (wa0[:, :], w_att[0:P]), (wa1[:, :], w_att[P:C]), (gbr[:, :], gb), (ww[:, :], w_w), (gate[0:64, 0, 0:12 * P], sel)]
        NL = 16 * len(LOADS)

        def run_chunks(eng, b, body):
            def place(k, n):
                return n if k < 2 else NCH - 1 - n
            for k in range(K):
                with eng.Fori(0, NCH // 2 - 1) as cc:
                    for e in range(2):
                        n = cc * 2 + e
                        body(k, place(k, n), e, b * G + n + k * NCH, k, place(k, n + 1), False)
                for n in (NCH - 2, NCH - 1):
                    nk, nn = (k, n + 1) if n + 1 < NCH else (k + 1, 0)
                    body(k, place(k, n), n % 2, b * G + (k * NCH + n), nk, place(nk, nn), nk == K)

        def run_project(eng, step):
            step(-1, 1, "n")
            step(0, 0, "np")
            step(1, 1, "np")
            step(2, 0, "npc")
            with eng.Fori(0, (NCH - 4) // 2) as cc:
                for e in range(2):
                    step(cc * 2 + (3 + e), (3 + e) % 2, "npcu")
            step(NCH - 1, 1, "pcu")
            step(NCH, 0, "cu")
            step(NCH + 1, 1, "cu")
            step(NCH + 2, 0, "u")

        def run_mix(eng, step):
            step(-1, 1, "n")
            step(0, 0, "np")
            with eng.Fori(0, (NCH - 4) // 2) as cc:
                for e in range(2):
                    step(cc * 2 + (1 + e), (1 + e) % 2, "np")
            step(NCH - 3, 1, "np")
            step(NCH - 2, 0, "np")
            step(NCH - 1, 1, "p")

        def run_attend(eng, attend):
            attend(0, 0, False, True)
            with eng.Fori(0, (NCH - 2) // 2) as cc:
                for e in range(2):
                    attend(cc * 2 + (1 + e), (1 + e) % 2, True, True)
            attend(NCH - 1, 1, True, False)

        TOPS = [0] + [1] * 10 + [2] * 3 + [0] * 2
        FIRST_TOP = [sum(TOPS[:m]) for m in range(MP)]
        assert sum(TOPS) == MP
        LAG = 2
        RB_AT, WY_AT, WR_AT = 4, 7, 9

        @block.sync
        def _(sp):
            for dst, src in LOADS:
                sp.dma_start(dst, src).then_inc(s_load, 16)
            sp.wait_ge(s_load, NL)
            barrier(sp, 0, -1)
            with sp.Fori(0, nb) as b:
                def loads(n):
                    with sp.Fori(0, NCH // 2) as cc:
                        for q in range(2):
                            i = (b * 2 + n) * NCH + cc * 2 + q
                            sp.wait_ge(S["x_free"], i + 1)
                            sl = bass.ds((cc * 2 + q) * T, T)
                            sp.dma_start(xa[:, q, :], xr[b, 0:P, sl]).then_inc(S[f"x_loaded{q}"], 16)
                            sp.dma_start(xb[:, q, :], xr[b, P:C, sl]).then_inc(S[f"x_loaded{q}"], 16)
                loads(0)
                barrier(sp, b, 0)
                barrier(sp, b, 1)
                loads(1)
                barrier(sp, b, 2)
                with sp.Fori(0, NCH) as c:
                    sp.wait_ge(S["fin_ready"], (b * NCH + c) * 2 + 4)
                    sl = bass.ds(c * T, T)
                    sp.dma_start(outr[b, 0:P, sl], fa[:, 0, :]).then_inc(S["out_stored"], 16)
                    sp.dma_start(outr[b, P:C, sl], fa[0:R, 1, :]).then_inc(S["out_stored"], 16)
                sp.wait_ge(S["out_stored"], b * (32 * NCH) + (32 * NCH + 32))
                barrier(sp, b, 3)

        @block.tensor
        def _(pe):
            mm = pe.matmul
            barrier(pe, 0, -1)

            def mean_of(bank, a, r, s):
                mm(ps[:, bank, :], avg[:, :], a, start=True, stop=False)
                mm(ps[:, bank, :], avg[0:R, :], r, start=False, stop=True).then_inc(S[s], 1)

            with pe.Fori(0, nb) as b:
                def two(bank, part):
                    w0 = slice(part * P, part * P + P)
                    mm(ps[:, bank, :], win0[:, w0], na[:, :], start=True, stop=False)
                    return mm(ps[:, bank, :], win1[:, w0], nb_[:, :], start=False, stop=True)

                def step(c, par, which):
                    i, j = b * NCH + c, b * NCH + (c + 1)
                    n = (b * 2) * NCH + (c + 1)
                    q = 1 - par
                    if "n" in which:
                        pe.wait_ge(S[f"x_loaded{q}"], (b * 2) * (16 * NCH) + (c + 1 - q) * 16 + 32)
                        mean_of(0, xa[:, q, :], xb[:, q, :], "mean_ready")
                    if "p" in which:
                        pe.wait_ge(S["norm_ready"], i * 2 + 4)
                        pe.wait_ge(S["gate_ready"], i + 1)
                        two(4, 2)
                        two(5, 3).then_inc(S["z_ready"], 1)
                    if "n" in which:
                        pe.wait_ge(S["sq_ready"], n * 2 + 2)
                        mean_of(1, sqa[:, :], sqb[:, :], "var_ready")
                    if "p" in which:
                        pe.wait_ge(S["tap_ready"], i * 2 + 2)
                        two(2, 0)
                        two(3, 1).then_inc(S["xc_ready"], 1)
                run_project(pe, step)
                barrier(pe, b, 0)

                def xdbl(k, c, g):
                    pe.wait_ge(S["xlo_ready"], g + 1)
                    order = k % 2
                    mm(flat(ps[0:64, 0, :]), wx0[:, k * 64:k * 64 + 64], chunk(u[:, 0], c, order), start=True, stop=False,
                       skip_group_check=True)
                    mm(flat(ps[0:64, 0, :]), wx1[:, k * 64:k * 64 + 64], chunk(u[:, 1], c, order), start=False,
                       stop=True, skip_group_check=True).then_inc(S["xdbl_ready"], 1)

                def dtproj(k, g):
                    pe.wait_ge(S["xd_ready"], g + 1)
                    pe.wait_ge(S["dt_ready"], g + 1)
                    for r in range(2):
                        m = mm(ps[:, 6 + r, :], wdt[:, (2 * k + r) * P:(2 * k + r + 1) * P], xd[:, :],
                               start=True, stop=True)
                    m.then_inc(S["dtpre_ready"], 1)

                def spread(what, q, par):
                    base = 0 if what == "B" else NT
                    bank = 2 if what == "B" else 4
                    for e in range(2):
                        j = base + 2 * q + e
                        m = mm(ps[:, bank + e, :], selr[:, j * P:(j + 1) * P], xhl[par][:, :], start=True, stop=True)
                    m.then_inc(S["bbc_ready" if what == "B" else "cbc_ready"], 1)

                def sumstates(q, g, s):
                    pe.wait_ge(S["hc_ready"], s + 2)
                    if q == 0:
                        pe.wait_ge(S["y_added"], g + 1)
                    for e in range(2):
                        if q < 2:
                            m = mm(ps[:, 1, :], eye[:, :], hc[:, e, :], start=(q == 0 and e == 0),
                                   stop=(q == 1 and e == 1))
                        else:
                            m = mm(ps[R:P, 0, :], foldw[:, :], hc[:, e, :], start=(e == 0), stop=(e == 1),
                                   skip_group_check=True)
                    m.then_inc(S["summed"], 1)

                def body(k, c, par, g, nk, ncx, last):
                    for q in range(NP):
                        s = g * NP + q
                        if q == 0 and not last:
                            xdbl(nk, ncx, g + 1)
                        if not (last and q == NP - 1):
                            if q == NP - 1:
                                pe.wait_ge(S["xlo_ready"], g + 3)
                            pe.wait_ge(S["bs_ready"], s + 2)
                            spread("B", (q + 1) % NP, par if q < NP - 1 else 1 - par)
                        pe.wait_ge(S["hc_ready"], s + 2)
                        spread("C", q, par)
                        if q > 0:
                            sumstates(q - 1, g, s)
                        if q == 0 and not last:
                            dtproj(nk, g + 1)
                    sumstates(NP - 1, g, g * NP + NP)

                g_0 = b * G
                xdbl(0, 0, g_0)
                dtproj(0, g_0)
                pe.wait_ge(S["xlo_ready"], g_0 + 2)
                spread("B", 0, 0)
                run_chunks(pe, b, body)
                barrier(pe, b, 1)

                def step(c, par, which):
                    i, j = b * NCH + c, b * NCH + (c + 1)
                    n = (b * 2 + 1) * NCH + (c + 1)
                    q = 1 - par
                    if "n" in which:
                        pe.wait_ge(S["yt_ready"], j + 1)
                        mean_of(0, pad0[:, bass.ds((c + 1) * T, T)], yt[:, q, :], "mean_ready")
                    if "p" in which:
                        pe.wait_ge(S["gated_ready"], i * 2 + 4)
                        for bank, lo, hi in ((2, 0, P), (3, P, C)):
                            mm(ps[0:hi - lo, bank, :], wo0[:, lo:hi], oa[:, :], start=True, stop=False)
                            m = mm(ps[0:hi - lo, bank, :], wo1[:, lo:hi], ob[:, :], start=False, stop=True)
                        m.then_inc(S["mixed"], 1)
                    if "n" in which:
                        pe.wait_ge(S["sq_ready"], n * 2 + 2)
                        mean_of(1, sqa[:, :], sqb[:, :], "var_ready")
                    if "p" in which:
                        pe.wait_ge(S["x1_ready"], i * 2 + 2)
                        pe.wait_ge(S["phl_ready"], i + 1)
                        mm(ps[0:O, 4, :], wa0[:, O:2 * O], na[:, :], start=True, stop=False)
                        mm(ps[0:O, 4, :], wa1[:, O:2 * O], nb_[:, :], start=False, stop=True)\
                            .then_inc(S["phi_ready"], 1)
                        pe.wait_ge(S["gtl_ready"], i + 1)
                        for t in range(T // P):
                            dst = ps[:, 5, t * P:t * P + O]
                            mm(dst, na[:, t * P:(t + 1) * P], wa0[:, 2 * O:3 * O], start=True, stop=False)
                            mm(dst, nb_[:, t * P:(t + 1) * P], wa1[:, 2 * O:3 * O], start=False, stop=False)
                            m = mm(dst, ones[0:1, :], gbr[:, :], start=False, stop=True)
                        m.then_inc(S["gt_ready"], 1)
                run_mix(pe, step)
                barrier(pe, b, 2)

                def theta(c, i, before):
                    if before:
                        pe.wait_ge(S["fin_ready"], i * 2 - 2)
                    mm(ps[0:O, 7, :], wa0[:, 0:O], pad0[:, bass.ds(c * T, T)], start=True, stop=False)
                    mm(ps[0:O, 7, :], wa1[:, 0:O], pad1[0:R, bass.ds(c * T, T)], start=False, stop=True)\
                        .then_inc(S["theta_ready"], 1)

                def top(j, i):
                    t, m = j // 4, j % 4
                    if j == 0:
                        pe.wait_ge(S["thh_ready"], i + 1)
                    pe.wait_ge(S["top_read"], i * MP + (j + 1))
                    for e in range(2):
                        mc = (2 * m + e) * T
                        q = mm(ps[:, 5 + e, :], thn[0][:, t * P:(t + 1) * P], phh[0:O, mc:mc + T],
                               start=True, stop=True)
                    q.then_inc(S["top_ready"], 1)

                def shift(i):
                    pe.wait_ge(S["nmx_ready"], i + 1)
                    for t in range(4):
                        q = mm(ps[O:O + 1, 7, t * P:(t + 1) * P], nmx[:, t:t + 1], eye[:, :], start=True, stop=True)
                    q.then_inc(S["shift_ready"], 1)

                def scores(mp, i, par):
                    s = i * MP + mp
                    if mp == 0:
                        pe.wait_ge(S["thc_ready"], i + 1)
                    pe.wait_ge(S["pf_ready"], s + 1)
                    for e in range(2):
                        m = 2 * mp + e
                        dst = ps[:, 2 * (mp % 2) + e, :]
                        kk = phh[:, m * P:(m + 1) * P]
                        mm(dst, kk, thc[par][0][:, :], start=True, stop=False)
                        mm(dst, phl[:, m * P:(m + 1) * P], thc[par][0][:, :], start=False, stop=False)
                        q = mm(dst, kk, thc[par][1][:, :], start=False, stop=True)
                    q.then_inc(S["st_ready"], 1)

                def weigh(mp, i):
                    s = i * MP + mp
                    pe.wait_ge(S["pl_ready"], s + 3)
                    if mp == 0:
                        pe.wait_ge(S["yraw_ready"], i + 1)
                    for e in range(2):
                        m = 2 * mp + e
                        dst = ps[0:O + 1, 4, :]
                        mm(dst, gth[:, m, :], ph[:, mp % 2, e, :], start=(m == 0), stop=False)
                        mm(dst, gtl[:, m, :], ph[:, mp % 2, e, :], start=False, stop=False)
                        q = mm(dst, gth[:, m, :], pl[:, mp % 2, e, :], start=False, stop=(m == MT - 1))
                    q.then_inc(S["pv_ready"], 1)

                def spread_den(i):
                    pe.wait_ge(S["rden_ready"], i + 1)
                    mm(ps[0:O, 7, :], ones[O:O + 1, 0:O], rden[O:O + 1, :], start=True, stop=True)\
                        .then_inc(S["rb_ready"], 1)

                def output(i, part):
                    if part == 0:
                        pe.wait_ge(S["yn_ready"], i + 2)
                    else:
                        pe.wait_ge(S["fin_ready"], i * 2 + 3)
                    lo, hi = ((0, P), (P, C))[part]
                    mm(ps[0:hi - lo, 7, :], ww[:, lo:hi], yn[:, :], start=True, stop=True).then_inc(S["wy_ready"], 1)

                i_0 = b * NCH

                def attend(c, par, before, nxt):
                    i = i_0 + c
                    for mp in range(MP):
                        scores(mp, i, par)
                        if mp == 0 and nxt:
                            theta(c + 1, i + 1, before)
                        if nxt:
                            for j in range(FIRST_TOP[mp], FIRST_TOP[mp] + TOPS[mp]):
                                top(j, i + 1)
                        if mp >= LAG:
                            weigh(mp - LAG, i)
                        elif before:
                            weigh(mp - LAG + MP, i - 1)
                        if before:
                            if mp == RB_AT:
                                if nxt:
                                    pe.wait_ge(S["thf_ready"], i + 2)
                                spread_den(i - 1)
                            if mp == WY_AT:
                                output(i - 1, 0)
                            if mp == WR_AT:
                                output(i - 1, 1)
                        if nxt and mp == MP - 2:
                            if before:
                                pe.wait_ge(S["fin_ready"], i * 2 + 2)
                            shift(i + 1)
                theta(0, i_0, False)
                for j in range(MP):
                    top(j, i_0)
                shift(i_0)
                run_attend(pe, attend)
                last = i_0 + (NCH - 1)
                for mp in range(MP - LAG, MP):
                    weigh(mp, last)
                spread_den(last)
                output(last, 0)
                output(last, 1)
                barrier(pe, b, 3)

        @block.scalar
        def _(act):
            A = act.activation
            act.preload_act_table_set("natural_log_exp_and_others")
            act.wait_ge(s_load, NL)
            A(selr[:, :], gate[0:64, 0, 0:12 * P], ACT.Copy)
            act.wait_ge(S["consts_set"], 1)
            A(negA[:, :], negA[:, :], ACT.Exp).then_inc(S["consts_set"], 1)
            barrier(act, 0, -1)
            with act.Fori(0, nb) as b:
                def squares(n):
                    act.wait_ge(S["dev_ready"], n * 2 + 2)
                    A(sqa[:, :], da[:, :], ACT.Square).then_inc(S["sq_ready"], 1)
                    A(sqb[:, :], db[:, :], ACT.Square).then_inc(S["sq_ready"], 1)

                def deviation(n):
                    act.wait_ge(S["var_ready"], n + 1)
                    A(lnv[:, :], ps[:, 1, :], ACT.Ln, bias=eps[:, :]).then_inc(S["rstd_ready"], 1)
                    act.wait_ge(S["rstd_ready"], n * 2 + 1)
                    A(rstd[:, :], lnv[:, :], ACT.Exp, scale=-0.5).then_inc(S["rstd_ready"], 1)

                def sigmoid(dst, src, name, at):
                    A(dst, src, ACT.Exp, scale=-1.0).then_inc(S[name], 1)
                    act.wait_ge(S[name], at + 1)
                    A(dst, dst, ACT.Ln, bias=1.0).then_inc(S[name], 1)
                    act.wait_ge(S[name], at + 2)
                    A(dst, dst, ACT.Exp, scale=-1.0).then_inc(S[name], 1)

                def step(c, par, which):
                    i, j = b * NCH + c, b * NCH + (c + 1)
                    n = (b * 2) * NCH + (c + 1)
                    if "n" in which:
                        squares(n)
                    if "u" in which:
                        w = b * NCH + (c - 3)
                        act.wait_ge(S["conv_ready"], w * 2 + 2)
                        act.wait_ge(S["u_ready"], w + 1)
                        sigmoid(cs[:, :, :], u[:, :, bass.ds((c - 3) * T, T)], "cs_ready", w * 3)
                    if "p" in which:
                        act.wait_ge(S["z_ready"], i + 1)
                        act.wait_ge(S["gate_ready"], i + 1)
                        sigmoid(zs[:, :, :], ps[:, 4:6, :], "zs_ready", i * 3)
                    if "n" in which:
                        deviation(n)
                    if "p" in which:
                        act.wait_ge(S["xc_ready"], i + 1)
                        for r in range(2):
                            A(padi[r][:, bass.ds(c * RPC + 1, RPC), 1:1 + WW], flat(ps[:, 2 + r, :]), ACT.Copy)\
                                .then_inc(S["pre_copied"], 1)
                        for r in range(2):
                            A(u[:, r, bass.ds(c * T, T)], ps[:, 2 + r, :], ACT.Identity,
                              bias=vecs[:, V_CB + r:V_CB + r + 1],
                              scale=vecs[:, V_TAP + 9 * r + 4:V_TAP + 9 * r + 5]).then_inc(S["tap_ready"], 1)
                run_project(act, step)
                barrier(act, b, 0)

                act.wait_ge(S["scan_set"], b + 1)

                def front_copy(par, g):
                    act.wait_ge(S["xdbl_ready"], g + 1)
                    act.wait_ge(S["dtpre_ready"], g + 1)
                    A(xd[0:NX, :], ps[0:NX, 0, :], ACT.Copy).then_inc(S["xd_ready"], 1)
                    act.wait_ge(S["summed"], g * NP + 1)
                    A(xhl[par][:, :], ps[0:64, 0, :], ACT.Copy).then_inc(S["xhi_ready"], 1)

                def front_soft(g):
                    act.wait_ge(S["dtpre_ready"], g + 2)
                    A(za[:, :, :], ps[:, 6:8, :], ACT.Abs).then_inc(S["soft_ready"], 1)
                    act.wait_ge(S["soft_ready"], g * 3 + 1)
                    A(za[:, :, :], za[:, :, :], ACT.Exp, scale=-1.0).then_inc(S["soft_ready"], 1)
                    act.wait_ge(S["soft_ready"], g * 3 + 2)
                    A(zl[:, :, :], za[:, :, :], ACT.Ln, bias=1.0).then_inc(S["soft_ready"], 1)

                def decay(k, q, s, g, slot):
                    if q == 0:
                        act.wait_ge(S["dt_ready"], g + 2)
                    act.wait_ge(S["hc_ready"], s + 1)
                    for e in range(2):
                        j = 2 * q + e
                        A(dA[:, slot, e, :], dt[:, 0 if j < NS else 1, :], ACT.Exp,
                          scale=negA[:, k * NT + j:k * NT + j + 1]).then_inc(S["dA_ready"], 1)
                    act.wait_ge(S["bbc_ready"], s + 1)
                    act.wait_ge(S["dbu_ready"], s + 1)
                    A(bs[:, slot, :, :], ps[:, 2:4, :], ACT.Copy).then_inc(S["bs_ready"], 1)

                def body(k, c, par, g, nk, ncx, last):
                    for q in range(NP):
                        s = g * NP + q
                        if q == 0 and not last:
                            front_copy(1 - par, g + 1)
                        if not (last and q == NP - 1):
                            decay(k if q < NP - 1 else nk, (q + 1) % NP, s + 1, g + (q == NP - 1),
                                  (par * NP + q + 1) % 2)
                        if q == 0 and not last:
                            front_soft(g + 1)
                g_0 = b * G
                front_copy(0, g_0)
                front_soft(g_0)
                decay(0, 0, g_0 * NP, g_0, 0)
                run_chunks(act, b, body)
                barrier(act, b, 1)

                def copy_rem(c, q):
                    A(yt[:, q, :], pad1[R:P, bass.ds(c * T, T)], ACT.Copy).then_inc(S["yt_ready"], 1)

                def step(c, par, which):
                    i, j = b * NCH + c, b * NCH + (c + 1)
                    n = (b * 2 + 1) * NCH + (c + 1)
                    if "n" in which:
                        squares(n)
                        deviation(n)
                    if "p" in which:
                        act.wait_ge(S["x1_ready"], i * 2 + 2)
                        A(pad0[:, bass.ds(c * T, T)], na[:, :], ACT.Copy)
                        A(pad1[0:R, bass.ds(c * T, T)], nb_[:, :], ACT.Copy)
                        act.wait_ge(S["phi_ready"], i + 1)
                        A(phf[:, :], ps[0:O, 4, :], ACT.Identity, bias=vecs[0:O, V_PB:V_PB + 1])\
                            .then_inc(S["phf_ready"], 1)
                        act.wait_ge(S["phf_ready"], i + 1)
                        A(phh[0:O, bass.ds(c * T, T)], phf[:, :], ACT.Copy).then_inc(S["phh_ready"], 1)
                        if not isinstance(c, int) or c + 2 < NCH:
                            copy_rem(c + 2, par)
                        act.wait_ge(S["gt_ready"], i + 1)
                        A(gth[:, bass.ds(c * 4, 4), 0:O], ps[:, 5, :].rearrange("p (t n) -> p t n", n=P)[:, :, 0:O],
                          ACT.Copy).then_inc(S["gth_ready"], 1)
                        act.wait_ge(S["phl_ready"], i + 2)
                act.wait_ge(S["att_set"], b * 4 + 4)
                copy_rem(0, 0)
                copy_rem(1, 1)
                run_mix(act, step)
                barrier(act, b, 2)

                def split_theta(i):
                    act.wait_ge(S["theta_ready"], i + 1)
                    A(thf[:, :], ps[0:O, 7, :], ACT.Identity, bias=vecs[0:O, V_TB:V_TB + 1])\
                        .then_inc(S["thf_ready"], 1)
                    act.wait_ge(S["thf_ready"], i + 1)
                    A(thn[0][:, :], thf[:, :], ACT.Copy).then_inc(S["thh_ready"], 1)

                def take_theta(i, par):
                    act.wait_ge(S["thl_ready"], i + 1)
                    A(thc[par][0][0:O, :], thn[0][:, :].bitcast(F32), ACT.Copy)
                    A(thc[par][1][0:O, :], thn[1][:, :].bitcast(F32), ACT.Copy)
                    act.wait_ge(S["shift_ready"], i + 1)
                    A(thc[par][0][O:O + 1, :], ps[O:O + 1, 7, :], ACT.Copy).then_inc(S["thc_ready"], 1)

                def read_sum(i):
                    act.wait_ge(S["pv_ready"], i * MP + (MP + 2))
                    act.wait_ge(S["yn_ready"], i + 1)
                    A(yraw[:, :], ps[0:O + 1, 4, :], ACT.Copy).then_inc(S["yraw_ready"], 1)

                i_0 = b * NCH

                def attend(c, par, before, nxt):
                    i = i_0 + c
                    for mp in range(MP):
                        s = i * MP + mp
                        act.wait_ge(S["st_ready"], s + 1)
                        act.wait_ge(S["pl_ready"], s + 1)
                        A(pf[:, mp % 2, :, :], ps[:, 2 * (mp % 2):2 * (mp % 2) + 2, :], ACT.Exp)\
                            .then_inc(S["pf_ready"], 1)
                        if mp == 0 and nxt:
                            split_theta(i + 1)
                        if mp == LAG and before:
                            read_sum(i - 1)
                        act.wait_ge(S["pf_ready"], s + 3)
                        act.wait_ge(S["pv_ready"], s + 1)
                        A(ph[:, mp % 2, :, :], pf[:, mp % 2, :, :], ACT.Copy).then_inc(S["ph_ready"], 1)
                        if mp == MP - 1 and nxt:
                            take_theta(i + 1, 1 - par)
                split_theta(i_0)
                act.wait_ge(S["thc_set"], b * 2 + 2)
                take_theta(i_0, 0)
                run_attend(act, attend)
                read_sum(i_0 + (NCH - 1))
                barrier(act, b, 3)

        @block.gpsimd
        def _(pool):
            pool.wait_ge(s_load, NL)
            pool.memset(avg[:, :], 1.0 / C)
            pool.memset(ones[:, :], 1.0)
            pool.memset(eps[:, :], 1e-5)
            barrier(pool, 0, -1)
            with pool.Fori(0, nb) as b:
                for t in padi:
                    for edge in (t[:, 0:1, :], t[:, PW - 1:PW, :], t[:, 1:PW - 1, 0:1], t[:, 1:PW - 1, PW - 1:PW]):
                        m = pool.memset(edge, 0.0)
                        m.then_inc(S["borders_set"], 1)

                def step(c, par, which):
                    j = b * NCH + (c + 1)
                    if "u" in which:
                        w = b * NCH + (c - 3)
                        pool.wait_ge(S["cs_ready"], w * 3 + 3)
                        sl = bass.ds((c - 3) * T, T)
                        pool.tensor_tensor(u[:, :, sl], u[:, :, sl], cs[:, :, :], ALU.mult).then_inc(S["u_ready"], 1)
                    if "n" in which:
                        pool.wait_ge(S["scaled"], j * 2 + 2)
                        if "p" in which:
                            pool.wait_ge(S["xc_ready"], j)
                        pool.sem_inc(mark, 1)
                        pool.tensor_scalar(na[:, :], da[:, :], vecs[:, V_LNW:V_LNW + 1], vecs[:, V_LNB:V_LNB + 1],
                                           ALU.mult, ALU.add).then_inc(S["norm_ready"], 1)
                        pool.tensor_scalar(nb_[:, :], db[:, :], vecs[0:R, V_LNW + 1:V_LNW + 2],
                                           vecs[0:R, V_LNB + 1:V_LNB + 2], ALU.mult, ALU.add)\
                            .then_inc(S["norm_ready"], 1)
                run_project(pool, step)
                barrier(pool, b, 0)

                def residue(g):
                    pool.wait_ge(S["res_ready"], g * 2 + 2)
                    pool.wait_ge(S["soft_ready"], g * 3 + 3)
                    pool.tensor_tensor(zl[:, :, :], zl[:, :, :], ze[:, :, :], ALU.add).then_inc(S["sp_ready"], 1)

                def times_u(k, c, g):
                    pool.wait_ge(S["dt_ready"], g + 2)
                    pool.wait_ge(S["dbu_ready"], g * NP + 2)
                    for r in range(2):
                        m = pool.tensor_tensor(flat(du[:, r, :]), flat(dt[:, r, :]), chunk(u[:, r], c, k % 2), ALU.mult)
                        m.then_inc(S["du_ready"], 1)
                    pool.wait_ge(S["du_ready"], g * 2 + 2)

                def drive(q, s, slot):
                    pool.wait_ge(S["bs_ready"], s + 2)
                    pool.wait_ge(S["hc_ready"], s + 1)
                    r = 0 if 2 * q < NS else 1
                    pool.tensor_tensor(dbu[:, slot, :, :], bs[:, slot, :, :],
                                       du[:, r:r + 1, :].to_broadcast([P, 2, T]), ALU.mult).then_inc(S["dbu_ready"], 1)

                def body(k, c, par, g, nk, ncx, last):
                    for q in range(NP):
                        s = g * NP + q
                        if q == NP - 1 and not last:
                            times_u(nk, ncx, g + 1)
                        if not (last and q == NP - 1):
                            drive((q + 1) % NP, s + 1, (par * NP + q + 1) % 2)
                        if q == 0 and not last:
                            residue(g + 1)
                g_0 = b * G
                residue(g_0)
                times_u(0, 0, g_0)
                drive(0, g_0 * NP, 0)
                run_chunks(pool, b, body)
                barrier(pool, b, 1)
                barrier(pool, b, 2)
                barrier(pool, b, 3)

        @block.vector
        def _(dve):
            TT, TS, STT = dve.tensor_tensor, dve.tensor_scalar, dve.scalar_tensor_tensor
            dve.wait_ge(s_load, NL)
            TS(negA[:, :], vecs[:, V_A:V_A + K * NT], ALOG_MAX, None, ALU.min).then_inc(S["consts_set"], 1)
            for r in range(2):
                dve.tensor_reduce(dsum[:, r:r + 1], vecs[:, V_DS + 4 * r:V_DS + 4 * r + 4], AX.X, ALU.add)
            dve.wait_ge(S["consts_set"], 2)
            TS(negA[:, :], negA[:, :], -1.0, None, ALU.mult)
            for name, n in (("x_free", 2), ("fin_ready", 2), ("gated_ready", 2), ("norm_ready", 2), ("gate_ready", 1), ("tap_ready", 2), ("u_ready", 1),
                            ("xlo_ready", 1), ("dt_ready", 1), ("hc_ready", 2), ("summed", 4), ("y_added", 1),
                            ("bs_ready", 1), ("dbu_ready", 2), ("dtpre_ready", 1), ("phl_ready", 1), ("gtl_ready", 1),
                            ("top_read", 1), ("pf_ready", 2), ("yraw_ready", 1), ("pv_ready", 2), ("pl_ready", 2),
                            ("yn_ready", 1), ("out_stored", 32)):
                dve.sem_inc(S[name], n)
            barrier(dve, 0, -1)

            def link(ins, name, n):
                ins.then_inc(S[name], 1)
                dve.wait_ge(S[name], n)

            with dve.Fori(0, nb) as b:
                def deviate(n, srca, srcb):
                    dve.wait_ge(S["mean_ready"], n + 1)
                    TT(da[:, :], srca, ps[:, 0, :], ALU.subtract).then_inc(S["dev_ready"], 1)
                    TT(db[:, :], srcb, ps[0:R, 0, :], ALU.subtract).then_inc(S["dev_ready"], 1)

                def convolve(r, c):
                    w = b * NCH + c
                    acc = chunk(u[:, r], c, 0)
                    n = 0
                    for t in range(9):
                        if t == 4:
                            continue
                        dy, dx = t // 3, t % 3
                        src = padi[r][:, bass.ds(c * RPC + dy, RPC), dx:dx + WW]
                        ins = STT(acc, src, vecs[:, V_TAP + 9 * r + t:V_TAP + 9 * r + t + 1], acc, ALU.mult, ALU.add)
                        n += 1
                        if n < 8:
                            link(ins, "conv_link", w * 14 + (r * 7 + n))
                    ins.then_inc(S["conv_ready"], 1)

                def step(c, par, which):
                    i, j = b * NCH + c, b * NCH + (c + 1)
                    n = (b * 2) * NCH + (c + 1)
                    q = 1 - par
                    if "n" in which:
                        dve.wait_ge(S["norm_ready"], j * 2 + 2)
                        deviate(n, xa[:, q, :], xb[:, q, :])
                        dve.wait_ge(S["dev_ready"], n * 2 + 2)
                        dve.sem_inc(S["x_free"], 1)
                    if "c" in which:
                        dve.wait_ge(S["borders_set"], b * 8 + 8)
                        if isinstance(c, int) and c > NCH:
                            dve.wait_ge(S["tap_ready"], (b * NCH + (c - 2)) * 2 + 4)
                        else:
                            dve.wait_ge(S["tap_ready"], (b * NCH + (c - 1)) * 2 + 4)
                        convolve(0, c - 2)
                    if "n" in which:
                        dve.wait_ge(S["rstd_ready"], n * 2 + 2)
                        TT(da[:, :], da[:, :], rstd[:, :], ALU.mult).then_inc(S["scaled"], 1)
                        TT(db[:, :], db[:, :], rstd[0:R, :], ALU.mult).then_inc(S["scaled"], 1)
                    if "p" in which:
                        dve.wait_ge(S["zs_ready"], i * 3 + 3)
                        TT(gate[:, :, bass.ds(c * T, T)], ps[:, 4:6, :], zs[:, :, :], ALU.mult)\
                            .then_inc(S["gate_ready"], 1)
                    if "c" in which:
                        convolve(1, c - 2)
                run_project(dve, step)
                barrier(dve, b, 0)

                dve.memset(xd[:, :], 1.0).then_inc(S["zero_h"], 1)
                dve.memset(h[:, 1, :, T - 1:T], 0.0).then_inc(S["zero_h"], 1)
                dve.wait_ge(S["zero_h"], b * (K + 1) + 2)
                dve.sem_inc(S["scan_set"], 1)

                def low_half(par, g):
                    dve.wait_ge(S["xhi_ready"], g + 1)
                    TT(xhl[par][LO:LO + 32, :], ps[LO:LO + 32, 0, :], xhl[par][LO:LO + 32, :].bitcast(F32),
                       ALU.subtract).then_inc(S["xlo_ready"], 1)

                def residue(g):
                    dve.wait_ge(S["soft_ready"], g * 3 + 2)
                    TS(ze[:, :, :], za[:, :, :], 1.0, -1.0, ALU.add, ALU.add).then_inc(S["res_ready"], 1)
                    dve.wait_ge(S["res_ready"], g * 2 + 1)
                    TT(ze[:, :, :], za[:, :, :], ze[:, :, :], ALU.subtract).then_inc(S["res_ready"], 1)

                def softplus(g):
                    dve.wait_ge(S["sp_ready"], g + 1)
                    STT(dt[:, :, :], ps[:, 6:8, :], 0.0, zl[:, :, :], ALU.max, ALU.add).then_inc(S["dt_ready"], 1)

                def scans(k, par, q, s, slot):
                    step = -1 if k >= 2 else 1
                    end = T - 1 if step == 1 else 0
                    dve.wait_ge(S["dA_ready"], s * 2 + 2)
                    dve.wait_ge(S["dbu_ready"], s + 3)
                    for e in range(2):
                        j = 2 * q + e
                        dve.tensor_tensor_scan(h[:, par, j, ::step], dA[:, slot, e, ::step], dbu[:, slot, e, ::step],
                                               h[:, 1 - par, j, end:end + 1], ALU.mult, ALU.add)\
                            .then_inc(S["scan_link"], 1)

                def times_c(par, q, s):
                    dve.wait_ge(S["scan_link"], s * 2 + 2)
                    dve.wait_ge(S["cbc_ready"], s + 1)
                    dve.wait_ge(S["summed"], s + 4)
                    TT(hc[:, :, :], h[:, par, 2 * q:2 * q + 2, :], ps[:, 4:6, :], ALU.mult).then_inc(S["hc_ready"], 1)

                def add_y(k, c, g):
                    dve.wait_ge(S["summed"], g * NP + (NP + 4))
                    if isinstance(c, int) or k >= 2:
                        dve.sem_inc(mark, 1)
                    for r, (lo, bank) in enumerate(((0, 1), (R, 0))):
                        y = chunk(Y[r], c, k % 2, lo, P)
                        if k == 0:
                            ins = STT(y, chunk(u[:, r], c, 0, lo, P), dsum[lo:P, r:r + 1], flat(ps[lo:P, bank, :]),
                                      ALU.mult, ALU.add)
                        else:
                            ins = TT(y, flat(ps[lo:P, bank, :]), y, ALU.add)
                    ins.then_inc(S["y_added"], 1)

                def body(k, c, par, g, nk, ncx, last):
                    for q in range(NP):
                        s = g * NP + q
                        scans(k, par, q, s, (par * NP + q) % 2)
                        times_c(par, q, s)
                        if q == 0 and not last:
                            low_half(1 - par, g + 1)
                            residue(g + 1)
                        if q == 1 and not last:
                            dve.wait_ge(S["dA_ready"], g * NT + NT)
                            dve.wait_ge(S["du_ready"], g * 2 + 2)
                            softplus(g + 1)
                    add_y(k, c, g)
                    if nk != k and not last:
                        end = T - 1 if nk < 2 else 0
                        dve.memset(h[:, par, :, end:end + 1], 0.0).then_inc(S["zero_h"], 1)
                        dve.wait_ge(S["zero_h"], b * (K + 1) + (k + 3))
                        dve.sem_inc(mark, 1)
                g_0 = b * G
                low_half(0, g_0)
                residue(g_0)
                softplus(g_0)
                run_chunks(dve, b, body)
                barrier(dve, b, 1)

                for t, v in ((phh[O:O + 1, :], 1.0), (phl[O:O + 1, :], 0.0), (gth[:, :, O:O + 1], 1.0),
                             (gtl[:, :, O:O + 1], 0.0)):
                    dve.memset(t.bitcast(F32), v).then_inc(S["att_set"], 1)

                def step(c, par, which):
                    i, j = b * NCH + c, b * NCH + (c + 1)
                    n = (b * 2 + 1) * NCH + (c + 1)
                    if "n" in which:
                        dve.wait_ge(S["gated_ready"], j * 2 + 2)
                        deviate(n, pad0[:, bass.ds((c + 1) * T, T)], yt[:, 1 - par, :])
                    if "p" in which:
                        dve.wait_ge(S["mixed"], i + 1)
                        dve.wait_ge(S[f"x_loaded{par}"], (b * 2 + 1) * (16 * NCH) + (c - par) * 16 + 32)
                        dve.wait_ge(S["gtl_ready"], i + 1)
                        TT(na[:, :], ps[:, 2, :], xa[:, par, :], ALU.add).then_inc(S["x1_ready"], 1)
                        TT(nb_[:, :], ps[0:R, 3, :], xb[:, par, :], ALU.add).then_inc(S["x1_ready"], 1)
                        dve.wait_ge(S["x1_ready"], i * 2 + 2)
                        dve.sem_inc(S["x_free"], 1)
                    if "n" in which:
                        dve.wait_ge(S["rstd_ready"], n * 2 + 2)
                        at = j * 4
                        link(TT(da[:, :], da[:, :], rstd[:, :], ALU.mult), "mix_link", at + 1)
                        link(TT(db[:, :], db[:, :], rstd[0:R, :], ALU.mult), "mix_link", at + 2)
                        link(TS(da[:, :], da[:, :], vecs[:, V_ONW:V_ONW + 1], vecs[:, V_ONB:V_ONB + 1],
                                ALU.mult, ALU.add), "mix_link", at + 3)
                        link(TS(db[:, :], db[:, :], vecs[0:R, V_ONW + 1:V_ONW + 2], vecs[0:R, V_ONB + 1:V_ONB + 2],
                                ALU.mult, ALU.add), "mix_link", at + 4)
                        sl = bass.ds((c + 1) * T, T)
                        TT(oa[:, :], da[:, :], gate[:, 0, sl], ALU.mult).then_inc(S["gated_ready"], 1)
                        TT(ob[:, :], db[:, :], gate[0:R, 1, sl], ALU.mult).then_inc(S["gated_ready"], 1)
                    if "p" in which:
                        sl = bass.ds(c * T, T)
                        dve.wait_ge(S["phh_ready"], i + 1)
                        TT(phl[0:O, sl], phf[:, :], phh[0:O, sl].bitcast(F32), ALU.subtract)\
                            .then_inc(S["phl_ready"], 1)
                        dve.wait_ge(S["gth_ready"], i + 1)
                        gs = bass.ds(c * 4, 4)
                        TT(gtl[:, gs, 0:O], ps[:, 5, :].rearrange("p (t n) -> p t n", n=P)[:, :, 0:O],
                           gth[:, gs, 0:O].bitcast(F32), ALU.subtract).then_inc(S["gtl_ready"], 1)
                run_mix(dve, step)
                barrier(dve, b, 2)

                def low_theta(i):
                    dve.wait_ge(S["thh_ready"], i + 1)
                    TT(thn[1][:, :], thf[:, :], thn[0][:, :].bitcast(F32), ALU.subtract).then_inc(S["thl_ready"], 1)

                def top(j, i):
                    dve.wait_ge(S["top_ready"], i * MP + (j + 1))
                    dve.tensor_reduce(mx[:, j // 4, j % 4:j % 4 + 1], ps[:, 5:7, :], AX.XY, ALU.max)\
                        .then_inc(S["top_read"], 1)

                def negate(i, first=False):
                    dve.wait_ge(S["top_read"], i * MP + MP + 1)
                    if not first:
                        dve.wait_ge(S["shift_ready"], i)
                    dve.tensor_reduce(nmx[:, :], mx[:, :, :], AX.X, ALU.max, negate=True).then_inc(S["nmx_ready"], 1)

                def low_exp(mp, s):
                    dve.wait_ge(S["ph_ready"], s + 1)
                    TT(pl[:, mp % 2, :, :], pf[:, mp % 2, :, :], ph[:, mp % 2, :, :].bitcast(F32), ALU.subtract)\
                        .then_inc(S["pl_ready"], 1)

                def invert(i):
                    dve.wait_ge(S["yraw_ready"], i + 2)
                    dve.reciprocal(rden[O:O + 1, :], yraw[O:O + 1, :]).then_inc(S["rden_ready"], 1)

                def divide(i):
                    dve.wait_ge(S["rb_ready"], i + 1)
                    TT(yn[:, :], yraw[0:O, :], ps[0:O, 7, :], ALU.mult).then_inc(S["yn_ready"], 1)

                def finish(c, i, part):
                    dve.wait_ge(S["wy_ready"], i * 2 + (part + 1))
                    if part == 0:
                        dve.wait_ge(S["out_stored"], i * 32 + 32)
                    hi = (P, R)[part]
                    STT(fa[0:hi, part, :], ps[0:hi, 7, :], vecs[0:hi, V_WB + part:V_WB + part + 1],
                        (pad0, pad1)[part][0:hi, bass.ds(c * T, T)], ALU.add, ALU.add).then_inc(S["fin_ready"], 1)

                i_0 = b * NCH

                def attend(c, par, before, nxt):
                    i = i_0 + c
                    for mp in range(MP):
                        if mp == 1 and nxt:
                            low_theta(i + 1)
                        if nxt:
                            for j in range(FIRST_TOP[mp], FIRST_TOP[mp] + TOPS[mp]):
                                top(j, i + 1)
                            if mp > 0 and FIRST_TOP[mp] == MP and FIRST_TOP[mp - 1] < MP:
                                negate(i + 1)
                        low_exp(mp, i * MP + mp)
                        if before:
                            if mp == LAG:
                                invert(i - 1)
                            if mp == RB_AT:
                                divide(i - 1)
                            if mp == WY_AT:
                                finish(c - 1, i - 1, 0)
                            if mp == WR_AT:
                                finish(c - 1, i - 1, 1)
                for q in range(2):
                    dve.memset(thc[q][1][O:O + 1, :].bitcast(F32), 0.0).then_inc(S["thc_set"], 1)
                low_theta(i_0)
                for j in range(MP):
                    top(j, i_0)
                negate(i_0, True)
                run_attend(dve, attend)
                last = i_0 + (NCH - 1)
                invert(last)
                divide(last)
                finish(NCH - 1, last, 0)
                finish(NCH - 1, last, 1)
                barrier(dve, b, 3)


def kernel(x, L0_conv_ln_w, L0_conv_ln_b, L0_conv_in_proj_w, L0_conv_conv_w, L0_conv_conv_b, L0_conv_x_proj_w,
           L0_conv_dt_proj_w, L0_conv_dt_proj_b, L0_conv_A_log, L0_conv_Ds, L0_conv_out_norm_w, L0_conv_out_norm_b,
           L0_conv_out_proj_w, L1_conv_g_w, L1_conv_g_b, L1_conv_theta_w, L1_conv_theta_b, L1_conv_phi_w,
           L1_conv_phi_b, L1_conv_W_w, L1_conv_W_b, _nb=B, _run=None):
    f = lambda a: np.ascontiguousarray(np.asarray(a))
    rem2 = lambda a: np.concatenate([a[..., P:C], a[..., P:C]], -1)

    vec = np.zeros((P, NV), np.float32)

    def put(col, v, twice=False):
        v = f(v)
        vec[:, col] = v[:P]
        vec[:, col + 1] = rem2(v)
    for col, v in ((V_LNW, L0_conv_ln_w), (V_LNB, L0_conv_ln_b), (V_CB, L0_conv_conv_b), (V_ONW, L0_conv_out_norm_w),
                   (V_ONB, L0_conv_out_norm_b), (V_WB, L1_conv_W_b)):
        put(col, v)
    ds, al, cw = f(L0_conv_Ds), f(L0_conv_A_log), f(L0_conv_conv_w).reshape(C, 9)
    for k in range(K):
        vec[:, V_DS + k], vec[:, V_DS + 4 + k] = ds[k, :P], rem2(ds[k])
        for n in range(NS):
            vec[:, V_A + k * NT + n] = al[k, :P, n]
        for m in range(NS // 2):
            vec[:, V_A + k * NT + NS + m] = np.concatenate([al[k, P:, 2 * m], al[k, P:, 2 * m + 1]])
    for t in range(9):
        vec[:, V_TAP + t], vec[:, V_TAP + 9 + t] = cw[:P, t], rem2(cw[:, t])
    vec[:O, V_TB], vec[:O, V_PB] = f(L1_conv_theta_b), f(L1_conv_phi_b)

    wi = f(L0_conv_in_proj_w).T
    w_in = np.concatenate([wi[:, :P], rem2(wi[:, :C]), wi[:, C:C + P], rem2(wi[:, C:])], 1)
    xp, dp, db = f(L0_conv_x_proj_w), f(L0_conv_dt_proj_w), f(L0_conv_dt_proj_b)
    w_x = np.zeros((2 * P, K * 64), np.float32)
    w_dt = np.zeros((NX + 1, K * 2 * P), np.float32)
    for k in range(K):
        w_x[:C, 64 * k:64 * k + NX] = w_x[:C, 64 * k + LO:64 * k + LO + NX] = xp[k].T
        both = np.concatenate([dp[k].T, np.zeros((2 * NS, C), np.float32), db[k][None]], 0)
        w_dt[:, 2 * k * P:(2 * k + 1) * P], w_dt[:, (2 * k + 1) * P:(2 * k + 2) * P] = both[:, :P], rem2(both)
    sel = np.zeros((64, 2 * NT, P), np.float32)
    for w in range(2):
        for j in range(NT):
            for p in range(P):
                n = j if j < NS else 2 * (j - NS) + p // R
                sel[RANK + w * NS + n, w * NT + j, p] = sel[LO + RANK + w * NS + n, w * NT + j, p] = 1.0
    arrays = {
        "x": f(x)[:_nb], "vec": vec, "w_in": w_in, "w_x": w_x, "w_dt": w_dt, "sel": sel.reshape(64, 2 * NT * P),
        "fold": np.concatenate([np.eye(R, dtype=np.float32)] * 2, 0), "ident": np.eye(P, dtype=np.float32),
        "w_out": f(L0_conv_out_proj_w).T,
        "w_att": np.concatenate([f(L1_conv_theta_w).T, f(L1_conv_phi_w).T, f(L1_conv_g_w).T], 1),
        "gb": f(L1_conv_g_b)[None], "w_w": f(L1_conv_W_w).T,
    }
    arrays = {f"in_{n}": np.ascontiguousarray(a) for n, a in arrays.items()}
    import concourse.bacc as bacc
    from concourse.bass_utils import run_bass_kernel_spmd
    nc = bacc.Bacc("TRN2", target_bir_lowering=False, num_devices=1)
    aps = [nc.dram_tensor(n, a.shape, F32, kind="ExternalInput").ap() for n, a in arrays.items()]
    res = nc.dram_tensor("out", [_nb, C, HH, WW], F32, kind="ExternalOutput").ap()
    build(nc, _nb, *aps, res)
    if _run:
        return _run(nc, arrays)
    return run_bass_kernel_spmd(nc, [arrays], core_ids=[0]).results[0]["out"]
```

```python
from contextlib import ExitStack

import numpy as np
import concourse.bass as bass
from concourse import mybir

F32 = mybir.dt.float32
F32R = mybir.dt.float32r
ALU = mybir.AluOpType
ACT = mybir.ActivationFunctionType
AX = mybir.AxisListType

B, C, HH, WW = 8, 192, 64, 64
L = HH * WW
P = 128
R = C - P
NS, RANK, K = 4, 12, 4
O = 96
T = 512
NCH = L // T
RPC = T // WW
NX = RANK + 2 * NS
NT = NS + NS // 2
NP = NT // 2
LO = 32
PW = WW + 2
G = K * NCH
MT = L // P
MP = MT // 2
NU = 4 * NCH
ALOG_MAX = 85.0

V_LNW, V_LNB, V_CB, V_DS, V_ONW, V_ONB, V_WB = 0, 2, 4, 6, 14, 16, 18
V_A, V_TAP, V_TB, V_PB, NV = 20, 44, 62, 63, 64


def build(nc, nb, x, vec, w_in, w_x, w_dt, sel, fold, ident, w_out, w_att, gb, w_w, out):
    xr = x.rearrange("b c h w -> b c (h w)")
    outr = out.rearrange("b c h w -> b c (h w)")
    ctx = ExitStack()
    with ctx:
        def sb(name, shape, dt=F32, where=ctx):
            return where.enter_context(nc.sbuf_tensor(name, shape, dt))

        def sem(name):
            return ctx.enter_context(nc.semaphore(name))

        pad0 = sb("pad0", [P, PW * PW])
        pad1 = sb("pad1", [P, PW * PW])
        gate = sb("gate", [P, 2, L])
        ux = ExitStack()
        u = sb("u", [P, 2, L], where=ux)
        ux.close()
        kx = ExitStack()
        phh = sb("phh", [O + 1, L], F32R, where=kx)
        phl = sb("phl", [O + 1, L], F32R, where=kx)
        ctx.push(kx)
        vecs = sb("vecs", [P, NV])
        negA = sb("negA", [P, K * NT])
        dsum = sb("dsum", [P, 2])
        eps = sb("eps", [P, 1])
        win0 = sb("win0", [P, 4 * P])
        win1 = sb("win1", [R, 4 * P])
        wx0 = sb("wx0", [P, K * 64])
        wx1 = sb("wx1", [P, K * 64])
        wdt = sb("wdt", [NX + 1, K * 2 * P])
        selr = sb("selr", [64, 12 * P], F32R)
        foldw = sb("foldw", [P, R])
        eye = sb("eye", [P, P])
        avg = sb("avg", [P, P])
        wo0 = sb("wo0", [P, C])
        wo1 = sb("wo1", [R, C])
        wa0 = sb("wa0", [P, 3 * O])
        wa1 = sb("wa1", [R, 3 * O])
        gbr = sb("gbr", [1, O])
        ww = sb("ww", [O, C])
        ones = sb("ones", [P, P])

        padi = [pad0[:, :].rearrange("p (h w) -> p h w", w=PW), pad1[:, :].rearrange("p (h w) -> p h w", w=PW)]
        Y = [pad0, pad1]

        def chunk(t, c, order, lo=0, hi=P):
            if order == 0:
                return t[lo:hi, bass.ds(c * T, T)].rearrange("p (a b) -> p a b", b=WW)
            return t[lo:hi, 0:L].rearrange("p (h w) -> p w h", w=WW)[:, bass.ds(c * RPC, RPC), :]

        def flat(ap):
            return ap.rearrange("p (a b) -> p a b", b=WW)

        vx = ExitStack()
        gth = sb("gth", [P, MT, O + 1], F32R, where=vx)
        gtl = sb("gtl", [P, MT, O + 1], F32R, where=vx)
        thf = sb("thf", [O, T], where=vx)
        thc = [[sb(f"thc{q}{i}", [O + 1, T], F32R, where=vx) for i in range(2)] for q in range(2)]
        mx = sb("mx", [P, 4, NU // 4], where=vx)
        lnx = ExitStack()
        xa = sb("xa", [P, 2, T], where=lnx)
        xb = sb("xb", [R, 2, T], where=lnx)
        da = sb("da", [P, T], where=lnx)
        db = sb("db", [R, T], where=lnx)
        sqa = sb("sqa", [P, T], where=lnx)
        sqb = sb("sqb", [R, T], where=lnx)
        lnv = sb("lnv", [P, T], where=lnx)
        rstd = sb("rstd", [P, T], where=lnx)
        na = sb("na", [P, T], where=lnx)
        nb_ = sb("nb", [R, T], where=lnx)
        oa = sb("oa", [P, T], where=lnx)
        ob = sb("ob", [R, T], where=lnx)
        yt = sb("yt", [R, 2, T], where=lnx)
        phf = sb("phf", [O, T], where=lnx)
        zs = sb("zs", [P, 2, T], where=lnx)
        cs = sb("cs", [P, 2, T], where=lnx)
        lnx.close()
        aty = ExitStack()
        pf = sb("pf", [P, 2, 2, T], where=aty)
        ph = sb("ph", [P, 2, 2, T], F32R, where=aty)
        pl = sb("pl", [P, 2, 2, T], F32R, where=aty)
        nmx = sb("nmx", [P, 4], where=aty)
        rcol = sb("rcol", [P, 4], where=aty)
        rbt = sb("rbt", [P, 4, O], where=aty)
        yraw = sb("yraw", [O + 1, T], where=aty)
        yn = sb("yn", [O, T], where=aty)
        fa = sb("fa", [P, 2, T], where=aty)
        aty.close()
        vx.close()
        scx = ExitStack()
        xd = sb("xd", [NX + 1, T], where=scx)
        xhl = [sb(f"xhl{i}", [64, T], F32R, where=scx) for i in range(2)]
        za = sb("za", [P, 2, T], where=scx)
        zl = sb("zl", [P, 2, T], where=scx)
        ze = sb("ze", [P, 2, T], where=scx)
        dt = sb("dt", [P, 2, T], where=scx)
        du = sb("du", [P, 2, T], where=scx)
        dA = sb("dA", [P, NP, 2, T], where=scx)
        bs = sb("bs", [P, NP, 2, T], where=scx)
        dbu = sb("dbu", [P, NP, 2, T], where=scx)
        h = sb("h", [P, NT, T], where=scx)
        hc = sb("hc", [P, NP, 2, T], where=scx)
        scx.close()

        ps = ctx.enter_context(nc.psum_tensor("ps", [P, 8, T], F32))

        s_load = sem("s_load")
        stage_done = sem("stage_done")
        mark = sem("mark")
        stages = 4

        def barrier(eng, b, n):
            eng.sem_inc(mark, 1)
            eng.drain().then_inc(stage_done, 1)
            eng.wait_ge(stage_done, b * (5 * stages) + (5 * (n + 1) + 5))
            eng.sem_inc(mark, 1)

        S = {n: sem(n) for n in (
            "consts_set", "borders_set", "scan_set", "att_set", "thc_set", "mx_link",
            "x_loaded0", "x_loaded1", "x_free", "mean_ready", "dev_ready", "sq_ready", "var_ready", "rstd_ready",
            "scaled", "norm_ready", "z_ready", "xc_ready", "zs_ready", "gate_ready", "tap_ready",
            "conv_link", "conv_ready", "cs_ready", "u_ready",
            "xdbl_ready", "xd_ready", "xhi_ready", "xlo_ready", "dtpre_ready", "soft_ready", "res_ready", "sp_ready",
            "dt_ready", "du_ready", "dA_ready", "bbc_ready", "bs_ready", "cbc_ready", "dbu_ready", "scan_link",
            "hc_ready", "summed", "y_added", "zero_h",
            "yt_ready", "mix_link", "gated_ready", "mixed", "x1_ready", "phi_ready", "phf_ready", "phh_ready", "phl_ready",
            "gt_ready", "gth_ready", "gtl_ready",
            "theta_ready", "thf_ready", "thh_ready", "thl_ready", "top_ready", "top_read", "nmx_ready", "shift_ready",
            "thc_ready", "st_ready", "pf_ready", "ph_ready", "pl_ready", "pv_ready", "yraw_ready", "den_ready", "inv_link", "rden_ready",
            "rb_ready", "yn_ready", "wy_ready", "fin_ready", "out_stored")}

        block = ctx.enter_context(nc.Block())
        LOADS = [(vecs[:, :], vec), (win0[:, :], w_in[0:P]), (win1[:, :], w_in[P:C]), (wx0[:, :], w_x[0:P]), (wx1[:, :], w_x[P:2 * P]),
                 (wdt[:, :], w_dt), (foldw[:, :], fold), (eye[:, :], ident), (wo0[:, :], w_out[0:P]), (wo1[:, :], w_out[P:C]),
                 (wa0[:, :], w_att[0:P]), (wa1[:, :], w_att[P:C]), (gbr[:, :], gb), (ww[:, :], w_w), (gate[0:64, 0, 0:12 * P], sel)]
        NL = 16 * len(LOADS)

        def run_chunks(eng, b, body):
            def place(k, n):
                if isinstance(n, int):
                    k, n = k + n // NCH, n % NCH
                    if not 0 <= k < K:
                        return None
                return k, (n if k < 2 else NCH - 1 - n)

            def one(k, n, e, at):
                body(k, e, b * G + (at + k * NCH), place(k, n - 1), place(k, n + 1), place(k, n + 2))
            for k in range(K):
                for n in (0, 1):
                    one(k, n, n, n)
                with eng.Fori(0, NCH // 2 - 2) as cc:
                    for e in range(2):
                        one(k, cc * 2 + (2 + e), e, cc * 2 + (2 + e))
                for n in (NCH - 2, NCH - 1):
                    one(k, n, n % 2, n)

        def run_project(eng, step):
            step(-1, 1, "n")
            step(0, 0, "np")
            step(1, 1, "np")
            step(2, 0, "npc")
            with eng.Fori(0, (NCH - 4) // 2) as cc:
                for e in range(2):
                    step(cc * 2 + (3 + e), (3 + e) % 2, "npcu")
            step(NCH - 1, 1, "pcu")
            step(NCH, 0, "cu")
            step(NCH + 1, 1, "cu")
            step(NCH + 2, 0, "u")

        def run_mix(eng, step):
            step(-1, 1, "n")
            step(0, 0, "np")
            with eng.Fori(0, (NCH - 4) // 2) as cc:
                for e in range(2):
                    step(cc * 2 + (1 + e), (1 + e) % 2, "np")
            step(NCH - 3, 1, "np")
            step(NCH - 2, 0, "np")
            step(NCH - 1, 1, "p")

        def run_attend(eng, attend):
            attend(0, 0, False, True)
            with eng.Fori(0, (NCH - 2) // 2) as cc:
                for e in range(2):
                    attend(cc * 2 + (1 + e), (1 + e) % 2, True, True)
            attend(NCH - 1, 1, True, False)

        TOPS = [0] + [2] * 7 + [3] * 6 + [0] * 2
        FIRST_TOP = [sum(TOPS[:m]) for m in range(MP)]
        assert sum(TOPS) == NU
        LAG = 2
        DEN_AT, RB_AT, WY_AT, WR_AT = 3, 4, 7, 9

        @block.sync
        def _(sp):
            for dst, src in LOADS:
                sp.dma_start(dst, src).then_inc(s_load, 16)
            sp.wait_ge(s_load, NL)
            barrier(sp, 0, -1)
            with sp.Fori(0, nb) as b:
                def loads(n):
                    with sp.Fori(0, NCH // 2) as cc:
                        for q in range(2):
                            i = (b * 2 + n) * NCH + cc * 2 + q
                            sp.wait_ge(S["x_free"], i + 1)
                            sl = bass.ds((cc * 2 + q) * T, T)
                            sp.dma_start(xa[:, q, :], xr[b, 0:P, sl]).then_inc(S[f"x_loaded{q}"], 16)
                            sp.dma_start(xb[:, q, :], xr[b, P:C, sl]).then_inc(S[f"x_loaded{q}"], 16)
                loads(0)
                barrier(sp, b, 0)
                barrier(sp, b, 1)
                loads(1)
                barrier(sp, b, 2)
                with sp.Fori(0, NCH) as c:
                    sp.wait_ge(S["fin_ready"], (b * NCH + c) * 2 + 4)
                    sl = bass.ds(c * T, T)
                    sp.dma_start(outr[b, 0:P, sl], fa[:, 0, :]).then_inc(S["out_stored"], 16)
                    sp.dma_start(outr[b, P:C, sl], fa[0:R, 1, :]).then_inc(S["out_stored"], 16)
                sp.wait_ge(S["out_stored"], b * (32 * NCH) + (32 * NCH + 32))
                barrier(sp, b, 3)

        @block.tensor
        def _(pe):
            mm = pe.matmul
            barrier(pe, 0, -1)

            def mean_of(bank, a, r, s):
                mm(ps[:, bank, :], avg[:, :], a, start=True, stop=False)
                mm(ps[:, bank, :], avg[0:R, :], r, start=False, stop=True).then_inc(S[s], 1)

            with pe.Fori(0, nb) as b:
                def two(bank, part):
                    w0 = slice(part * P, part * P + P)
                    mm(ps[:, bank, :], win0[:, w0], na[:, :], start=True, stop=False)
                    return mm(ps[:, bank, :], win1[:, w0], nb_[:, :], start=False, stop=True)

                def step(c, par, which):
                    i, j = b * NCH + c, b * NCH + (c + 1)
                    n = (b * 2) * NCH + (c + 1)
                    q = 1 - par
                    if "n" in which:
                        pe.wait_ge(S[f"x_loaded{q}"], (b * 2) * (16 * NCH) + (c + 1 - q) * 16 + 32)
                        mean_of(0, xa[:, q, :], xb[:, q, :], "mean_ready")
                    if "p" in which:
                        pe.wait_ge(S["norm_ready"], i * 2 + 4)
                        pe.wait_ge(S["gate_ready"], i + 1)
                        two(4, 2)
                        two(5, 3).then_inc(S["z_ready"], 1)
                    if "n" in which:
                        pe.wait_ge(S["sq_ready"], n * 2 + 2)
                        mean_of(1, sqa[:, :], sqb[:, :], "var_ready")
                    if "p" in which:
                        pe.wait_ge(S["tap_ready"], i * 2 + 2)
                        two(2, 0)
                        two(3, 1).then_inc(S["xc_ready"], 1)
                run_project(pe, step)
                barrier(pe, b, 0)

                def xdbl(k, c, g):
                    pe.wait_ge(S["xlo_ready"], g + 1)
                    order = k % 2
                    mm(flat(ps[0:64, 0, :]), wx0[:, k * 64:k * 64 + 64], chunk(u[:, 0], c, order), start=True, stop=False,
                       skip_group_check=True)
                    mm(flat(ps[0:64, 0, :]), wx1[:, k * 64:k * 64 + 64], chunk(u[:, 1], c, order), start=False,
                       stop=True, skip_group_check=True).then_inc(S["xdbl_ready"], 1)

                def dtproj(k, g):
                    pe.wait_ge(S["xd_ready"], g + 1)
                    pe.wait_ge(S["dt_ready"], g + 1)
                    for r in range(2):
                        m = mm(ps[:, 6 + r, :], wdt[:, (2 * k + r) * P:(2 * k + r + 1) * P], xd[:, :],
                               start=True, stop=True)
                    m.then_inc(S["dtpre_ready"], 1)

                def spread(what, q, par):
                    base = 0 if what == "B" else NT
                    bank = 2 if what == "B" else 4
                    for e in range(2):
                        j = base + 2 * q + e
                        m = mm(ps[:, bank + e, :], selr[:, j * P:(j + 1) * P], xhl[par][:, :], start=True, stop=True)
                    m.then_inc(S["bbc_ready" if what == "B" else "cbc_ready"], 1)

                def sumstates(q, g, s):
                    pe.wait_ge(S["hc_ready"], s + 3)
                    if q == 0:
                        pe.wait_ge(S["y_added"], g + 1)
                    for e in range(2):
                        if q < 2:
                            m = mm(ps[:, 1, :], eye[:, :], hc[:, q, e, :], start=(q == 0 and e == 0),
                                   stop=(q == 1 and e == 1))
                        else:
                            m = mm(ps[R:P, 0, :], foldw[:, :], hc[:, q, e, :], start=(e == 0), stop=(e == 1),
                                   skip_group_check=True)
                    m.then_inc(S["summed"], 1)

                def body(k, par, g, before, nxt, after):
                    for q in range(NP):
                        s = g * NP + q
                        if q == 0 or nxt:
                            if q == 1:
                                pe.wait_ge(S["xlo_ready"], g + 3)
                            pe.wait_ge(S["bs_ready"], s + 3)
                            spread("B", (q + 2) % NP, par if q == 0 else 1 - par)
                        pe.wait_ge(S["hc_ready"], s + 3)
                        spread("C", q, par)
                        if q == 1 and after:
                            dtproj(after[0], g + 2)
                        if q == 0 and before:
                            sumstates(1, g, s - 1)
                            sumstates(NP - 1, g, s)
                        if q == 2:
                            sumstates(0, g, s - 1)
                        if q == 0 and after:
                            xdbl(*after, g + 2)

                g_0 = b * G
                xdbl(0, 0, g_0)
                dtproj(0, g_0)
                xdbl(0, 1, g_0 + 1)
                spread("B", 0, 0)
                pe.wait_ge(S["bs_ready"], g_0 * NP + 2)
                spread("B", 1, 0)
                dtproj(0, g_0 + 1)
                run_chunks(pe, b, body)
                sumstates(1, g_0 + G - 1, (g_0 + G) * NP - 1)
                sumstates(NP - 1, g_0 + G - 1, (g_0 + G) * NP)
                barrier(pe, b, 1)

                i_0 = b * NCH

                def theta_of(xa_, xb_):
                    mm(ps[0:O, 7, :], wa0[:, 0:O], xa_, start=True, stop=False)
                    mm(ps[0:O, 7, :], wa1[:, 0:O], xb_, start=False, stop=True).then_inc(S["theta_ready"], 1)

                def top(j, i, par, t, m, bank):
                    if j == 0:
                        pe.wait_ge(S["thh_ready"], i + 1)
                    pe.wait_ge(S["top_read"], i * NU + (j + 1))
                    mm(ps[:, bank, :], thc[par][0][0:O, t * P:(t + 1) * P], phh[0:O, bass.ds(m * T, T)],
                       start=True, stop=True).then_inc(S["top_ready"], 1)

                def early_top(c, t):
                    m = c - 1
                    if t == 0:
                        pe.wait_ge(S["phh_ready"], i_0 + c)
                        pe.wait_ge(S["thh_ready"], i_0 + 1)
                    pe.wait_ge(S["top_read"], i_0 * NU + m * 4 + (t + 1))
                    mm(ps[:, 6 + t % 2, :], thc[0][0][0:O, t * P:(t + 1) * P], phh[0:O, bass.ds(m * T, T)],
                       start=True, stop=True).then_inc(S["top_ready"], 1)

                def step(c, par, which):
                    i, j = b * NCH + c, b * NCH + (c + 1)
                    n = (b * 2 + 1) * NCH + (c + 1)
                    q = 1 - par
                    if "n" in which:
                        pe.wait_ge(S["yt_ready"], j + 1)
                        mean_of(0, pad0[:, bass.ds((c + 1) * T, T)], yt[:, q, :], "mean_ready")
                    if "p" in which:
                        pe.wait_ge(S["gated_ready"], i * 2 + 4)
                        for bank, lo, hi in ((2, 0, P), (3, P, C)):
                            mm(ps[0:hi - lo, bank, :], wo0[:, lo:hi], oa[:, :], start=True, stop=False)
                            m = mm(ps[0:hi - lo, bank, :], wo1[:, lo:hi], ob[:, :], start=False, stop=True)
                        m.then_inc(S["mixed"], 1)
                    if "n" in which:
                        pe.wait_ge(S["sq_ready"], n * 2 + 2)
                        mean_of(1, sqa[:, :], sqb[:, :], "var_ready")
                    early = "p" in which and not (isinstance(c, int) and c == 0)
                    if early:
                        early_top(c, 0)
                        early_top(c, 1)
                    if "p" in which:
                        pe.wait_ge(S["x1_ready"], i * 2 + 2)
                        pe.wait_ge(S["phl_ready"], i + 1)
                        mm(ps[0:O, 4, :], wa0[:, O:2 * O], na[:, :], start=True, stop=False)
                        mm(ps[0:O, 4, :], wa1[:, O:2 * O], nb_[:, :], start=False, stop=True)\
                            .then_inc(S["phi_ready"], 1)
                        if not early:
                            theta_of(na[:, :], nb_[:, :])
                        pe.wait_ge(S["gtl_ready"], i + 1)
                        for t in range(T // P):
                            dst = ps[:, 5, t * P:t * P + O]
                            mm(dst, na[:, t * P:(t + 1) * P], wa0[:, 2 * O:3 * O], start=True, stop=False)
                            mm(dst, nb_[:, t * P:(t + 1) * P], wa1[:, 2 * O:3 * O], start=False, stop=False)
                            m = mm(dst, ones[0:1, :], gbr[:, :], start=False, stop=True)
                        m.then_inc(S["gt_ready"], 1)
                    if early:
                        early_top(c, 2)
                        early_top(c, 3)
                run_mix(pe, step)
                barrier(pe, b, 2)

                def theta(c, i, before):
                    if before:
                        pe.wait_ge(S["fin_ready"], i * 2 - 2)
                    theta_of(pad0[:, bass.ds(c * T, T)], pad1[0:R, bass.ds(c * T, T)])

                def shift(i):
                    pe.wait_ge(S["nmx_ready"], i + 1)
                    for t in range(4):
                        q = mm(ps[O:O + 1, 7, t * P:(t + 1) * P], nmx[:, t:t + 1], eye[:, :], start=True, stop=True)
                    q.then_inc(S["shift_ready"], 1)

                def scores(mp, i, par):
                    s = i * MP + mp
                    if mp == 0:
                        pe.wait_ge(S["thc_ready"], i + 1)
                    pe.wait_ge(S["pf_ready"], s + 1)
                    for e in range(2):
                        m = 2 * mp + e
                        dst = ps[:, 2 * (mp % 2) + e, :]
                        kk = phh[:, m * P:(m + 1) * P]
                        mm(dst, kk, thc[par][0][:, :], start=True, stop=False)
                        mm(dst, phl[:, m * P:(m + 1) * P], thc[par][0][:, :], start=False, stop=False)
                        q = mm(dst, kk, thc[par][1][:, :], start=False, stop=True)
                    q.then_inc(S["st_ready"], 1)

                def weigh(mp, i):
                    s = i * MP + mp
                    pe.wait_ge(S["pl_ready"], s + 3)
                    if mp == 0:
                        pe.wait_ge(S["yraw_ready"], i + 1)
                    for e in range(2):
                        m = 2 * mp + e
                        dst = ps[0:O + 1, 4, :]
                        mm(dst, gth[:, m, :], ph[:, mp % 2, e, :], start=(m == 0), stop=False)
                        mm(dst, gtl[:, m, :], ph[:, mp % 2, e, :], start=False, stop=False)
                        q = mm(dst, gth[:, m, :], pl[:, mp % 2, e, :], start=False, stop=(m == MT - 1))
                    q.then_inc(S["pv_ready"], 1)

                def turn_den(i):
                    pe.wait_ge(S["yraw_ready"], i + 2)
                    for t in range(4):
                        q = mm(ps[:, 7, t:t + 1], yraw[O:O + 1, t * P:(t + 1) * P], ones[O:O + 1, 0:1],
                               start=True, stop=True)
                    q.then_inc(S["den_ready"], 1)

                def spread_den(i):
                    pe.wait_ge(S["rden_ready"], i + 1)
                    for t in range(4):
                        q = mm(ps[0:O, 7, t * P:(t + 1) * P], rbt[:, t, :], eye[:, :], start=True, stop=True)
                    q.then_inc(S["rb_ready"], 1)

                def output(i, part):
                    if part == 0:
                        pe.wait_ge(S["yn_ready"], i + 2)
                    else:
                        pe.wait_ge(S["fin_ready"], i * 2 + 3)
                    lo, hi = ((0, P), (P, C))[part]
                    mm(ps[0:hi - lo, 7, :], ww[:, lo:hi], yn[:, :], start=True, stop=True).then_inc(S["wy_ready"], 1)

                i_0 = b * NCH

                def attend(c, par, before, nxt):
                    i = i_0 + c
                    for mp in range(MP):
                        scores(mp, i, par)
                        if mp == 0 and nxt:
                            theta(c + 1, i + 1, before)
                        blocks = range(FIRST_TOP[mp], FIRST_TOP[mp] + TOPS[mp]) if nxt else ()
                        for j in blocks[:2]:
                            top(j, i + 1, 1 - par, j // (NU // 4), j % (NU // 4), 5 + j % 2)
                        if mp >= LAG:
                            weigh(mp - LAG, i)
                        elif before:
                            weigh(mp - LAG + MP, i - 1)
                        for j in blocks[2:]:
                            top(j, i + 1, 1 - par, j // (NU // 4), j % (NU // 4), 5 + j % 2)
                        if before:
                            if mp == DEN_AT:
                                if nxt:
                                    pe.wait_ge(S["thf_ready"], i + 2)
                                turn_den(i - 1)
                            if mp == RB_AT:
                                spread_den(i - 1)
                            if mp == WY_AT:
                                output(i - 1, 0)
                            if mp == WR_AT:
                                output(i - 1, 1)
                        if nxt and mp == MP - 2:
                            if before:
                                pe.wait_ge(S["fin_ready"], i * 2 + 2)
                            shift(i + 1)
                for t in range(4):
                    top(NU - 4 + t, i_0, 0, t, NCH - 1, 5 + t % 2)
                shift(i_0)
                run_attend(pe, attend)
                last = i_0 + (NCH - 1)
                for mp in range(MP - LAG, MP):
                    weigh(mp, last)
                turn_den(last)
                spread_den(last)
                output(last, 0)
                output(last, 1)
                barrier(pe, b, 3)

        @block.scalar
        def _(act):
            A = act.activation
            act.preload_act_table_set("natural_log_exp_and_others")
            act.wait_ge(s_load, NL)
            A(selr[:, :], gate[0:64, 0, 0:12 * P], ACT.Copy)
            act.wait_ge(S["consts_set"], 1)
            A(negA[:, :], negA[:, :], ACT.Exp).then_inc(S["consts_set"], 1)
            barrier(act, 0, -1)
            with act.Fori(0, nb) as b:
                def squares(n):
                    act.wait_ge(S["dev_ready"], n * 2 + 2)
                    A(sqa[:, :], da[:, :], ACT.Square).then_inc(S["sq_ready"], 1)
                    A(sqb[:, :], db[:, :], ACT.Square).then_inc(S["sq_ready"], 1)

                def deviation(n):
                    act.wait_ge(S["var_ready"], n + 1)
                    A(lnv[:, :], ps[:, 1, :], ACT.Ln, bias=eps[:, :]).then_inc(S["rstd_ready"], 1)
                    act.wait_ge(S["rstd_ready"], n * 2 + 1)
                    A(rstd[:, :], lnv[:, :], ACT.Exp, scale=-0.5).then_inc(S["rstd_ready"], 1)

                def sigmoid(dst, src, name, at):
                    A(dst, src, ACT.Exp, scale=-1.0).then_inc(S[name], 1)
                    act.wait_ge(S[name], at + 1)
                    A(dst, dst, ACT.Ln, bias=1.0).then_inc(S[name], 1)
                    act.wait_ge(S[name], at + 2)
                    A(dst, dst, ACT.Exp, scale=-1.0).then_inc(S[name], 1)

                def step(c, par, which):
                    i, j = b * NCH + c, b * NCH + (c + 1)
                    n = (b * 2) * NCH + (c + 1)
                    if "n" in which:
                        squares(n)
                    if "u" in which:
                        w = b * NCH + (c - 3)
                        act.wait_ge(S["conv_ready"], w * 2 + 2)
                        act.wait_ge(S["u_ready"], w + 1)
                        sigmoid(cs[:, :, :], u[:, :, bass.ds((c - 3) * T, T)], "cs_ready", w * 3)
                    if "p" in which:
                        act.wait_ge(S["z_ready"], i + 1)
                        act.wait_ge(S["gate_ready"], i + 1)
                        sigmoid(zs[:, :, :], ps[:, 4:6, :], "zs_ready", i * 3)
                    if "n" in which:
                        deviation(n)
                    if "p" in which:
                        act.wait_ge(S["xc_ready"], i + 1)
                        for r in range(2):
                            A(padi[r][:, bass.ds(c * RPC + 1, RPC), 1:1 + WW], flat(ps[:, 2 + r, :]), ACT.Copy)
                        for r in range(2):
                            A(u[:, r, bass.ds(c * T, T)], ps[:, 2 + r, :], ACT.Identity,
                              bias=vecs[:, V_CB + r:V_CB + r + 1],
                              scale=vecs[:, V_TAP + 9 * r + 4:V_TAP + 9 * r + 5]).then_inc(S["tap_ready"], 1)
                run_project(act, step)
                barrier(act, b, 0)

                act.wait_ge(S["scan_set"], b + 1)

                def copy_xd(g):
                    act.wait_ge(S["xdbl_ready"], g + 1)
                    act.wait_ge(S["dtpre_ready"], g + 1)
                    A(xd[0:NX, :], ps[0:NX, 0, :], ACT.Copy).then_inc(S["xd_ready"], 1)

                def copy_high(par, g):
                    act.wait_ge(S["cbc_ready"], g * NP + 1)
                    A(xhl[par][:, :], ps[0:64, 0, :], ACT.Copy).then_inc(S["xhi_ready"], 1)

                def front_soft(g):
                    act.wait_ge(S["dtpre_ready"], g + 2)
                    A(za[:, :, :], ps[:, 6:8, :], ACT.Abs).then_inc(S["soft_ready"], 1)
                    act.wait_ge(S["soft_ready"], g * 3 + 1)
                    A(za[:, :, :], za[:, :, :], ACT.Exp, scale=-1.0).then_inc(S["soft_ready"], 1)
                    act.wait_ge(S["soft_ready"], g * 3 + 2)
                    A(zl[:, :, :], za[:, :, :], ACT.Ln, bias=1.0).then_inc(S["soft_ready"], 1)

                def decay(k, q, s, g):
                    act.wait_ge(S["bbc_ready"], s + 1)
                    act.wait_ge(S["dbu_ready"], s + 1)
                    A(bs[:, q, :, :], ps[:, 2:4, :], ACT.Copy).then_inc(S["bs_ready"], 1)
                    if q == 0:
                        act.wait_ge(S["dt_ready"], g + 2)
                    act.wait_ge(S["hc_ready"], s + 1)
                    for e in range(2):
                        j = 2 * q + e
                        A(dA[:, q, e, :], dt[:, 0 if j < NS else 1, :], ACT.Exp,
                          scale=negA[:, k * NT + j:k * NT + j + 1]).then_inc(S["dA_ready"], 1)

                def body(k, par, g, before, nxt, after):
                    for q in range(NP):
                        s = g * NP + q
                        if q == 0 and nxt:
                            copy_high(1 - par, g + 1)
                        if q == 0:
                            decay(k, NP - 1, s + 2, g)
                        elif nxt:
                            decay(nxt[0], q - 1, s + 2, g + 1)
                        if q == 0 and after:
                            copy_xd(g + 2)
                        if q == 1 and after:
                            front_soft(g + 2)
                g_0 = b * G
                copy_xd(g_0)
                copy_high(0, g_0)
                front_soft(g_0)
                decay(0, 0, g_0 * NP, g_0)
                copy_xd(g_0 + 1)
                decay(0, 1, g_0 * NP + 1, g_0)
                front_soft(g_0 + 1)
                run_chunks(act, b, body)
                barrier(act, b, 1)

                def split_theta(i, par):
                    act.wait_ge(S["theta_ready"], i + 1)
                    A(thf[:, :], ps[0:O, 7, :], ACT.Identity, bias=vecs[0:O, V_TB:V_TB + 1])\
                        .then_inc(S["thf_ready"], 1)
                    act.wait_ge(S["thf_ready"], i + 1)
                    A(thc[par][0][0:O, :], thf[:, :], ACT.Copy).then_inc(S["thh_ready"], 1)

                def copy_rem(c, q):
                    A(yt[:, q, :], pad1[R:P, bass.ds(c * T, T)], ACT.Copy).then_inc(S["yt_ready"], 1)

                def step(c, par, which):
                    i, j = b * NCH + c, b * NCH + (c + 1)
                    n = (b * 2 + 1) * NCH + (c + 1)
                    if "n" in which:
                        squares(n)
                        deviation(n)
                    if "p" in which:
                        act.wait_ge(S["x1_ready"], i * 2 + 2)
                        A(pad0[:, bass.ds(c * T, T)], na[:, :], ACT.Copy)
                        A(pad1[0:R, bass.ds(c * T, T)], nb_[:, :], ACT.Copy)
                        act.wait_ge(S["phi_ready"], i + 1)
                        A(phf[:, :], ps[0:O, 4, :], ACT.Identity, bias=vecs[0:O, V_PB:V_PB + 1])\
                            .then_inc(S["phf_ready"], 1)
                        act.wait_ge(S["phf_ready"], i + 1)
                        A(phh[0:O, bass.ds(c * T, T)], phf[:, :], ACT.Copy).then_inc(S["phh_ready"], 1)
                        if not isinstance(c, int) or c + 2 < NCH:
                            copy_rem(c + 2, par)
                        act.wait_ge(S["gt_ready"], i + 1)
                        A(gth[:, bass.ds(c * 4, 4), 0:O], ps[:, 5, :].rearrange("p (t n) -> p t n", n=P)[:, :, 0:O],
                          ACT.Copy).then_inc(S["gth_ready"], 1)
                        act.wait_ge(S["phl_ready"], i + 2)
                        if isinstance(c, int) and c == 0:
                            split_theta(i, 0)
                copy_rem(0, 0)
                copy_rem(1, 1)
                run_mix(act, step)
                barrier(act, b, 2)

                def take_shift(i, par):
                    act.wait_ge(S["thl_ready"], i + 1)
                    act.wait_ge(S["shift_ready"], i + 1)
                    A(thc[par][0][O:O + 1, :], ps[O:O + 1, 7, :], ACT.Copy).then_inc(S["thc_ready"], 1)

                def read_sum(i):
                    act.wait_ge(S["pv_ready"], i * MP + (MP + 2))
                    act.wait_ge(S["yn_ready"], i + 1)
                    A(yraw[:, :], ps[0:O + 1, 4, :], ACT.Copy).then_inc(S["yraw_ready"], 1)

                i_0 = b * NCH

                def attend(c, par, before, nxt):
                    i = i_0 + c
                    for mp in range(MP):
                        s = i * MP + mp
                        if mp == MP - 1 and nxt:
                            take_shift(i + 1, 1 - par)
                        act.wait_ge(S["st_ready"], s + 1)
                        act.wait_ge(S["pl_ready"], s + 1)
                        A(pf[:, mp % 2, :, :], ps[:, 2 * (mp % 2):2 * (mp % 2) + 2, :], ACT.Exp)\
                            .then_inc(S["pf_ready"], 1)
                        if mp == 0 and nxt:
                            split_theta(i + 1, 1 - par)
                        if mp == LAG and before:
                            read_sum(i - 1)
                        act.wait_ge(S["pf_ready"], s + 3)
                        act.wait_ge(S["pv_ready"], s + 1)
                        A(ph[:, mp % 2, :, :], pf[:, mp % 2, :, :], ACT.Copy).then_inc(S["ph_ready"], 1)
                act.wait_ge(S["thc_set"], b * 2 + 2)
                take_shift(i_0, 0)
                run_attend(act, attend)
                read_sum(i_0 + (NCH - 1))
                barrier(act, b, 3)

        @block.gpsimd
        def _(pool):
            pool.wait_ge(s_load, NL)
            pool.memset(avg[:, :], 1.0 / C)
            pool.memset(ones[:, :], 1.0)
            pool.memset(eps[:, :], 1e-5)
            barrier(pool, 0, -1)
            with pool.Fori(0, nb) as b:
                for t in padi:
                    for edge in (t[:, 0:1, :], t[:, PW - 1:PW, :], t[:, 1:PW - 1, 0:1], t[:, 1:PW - 1, PW - 1:PW]):
                        m = pool.memset(edge, 0.0)
                        m.then_inc(S["borders_set"], 1)

                def step(c, par, which):
                    j = b * NCH + (c + 1)
                    if "u" in which:
                        w = b * NCH + (c - 3)
                        pool.wait_ge(S["cs_ready"], w * 3 + 3)
                        sl = bass.ds((c - 3) * T, T)
                        pool.tensor_tensor(u[:, :, sl], u[:, :, sl], cs[:, :, :], ALU.mult).then_inc(S["u_ready"], 1)
                    if "n" in which:
                        pool.wait_ge(S["scaled"], j * 2 + 2)
                        if "p" in which:
                            pool.wait_ge(S["xc_ready"], j)
                        pool.sem_inc(mark, 1)
                        pool.tensor_scalar(na[:, :], da[:, :], vecs[:, V_LNW:V_LNW + 1], vecs[:, V_LNB:V_LNB + 1],
                                           ALU.mult, ALU.add).then_inc(S["norm_ready"], 1)
                        pool.tensor_scalar(nb_[:, :], db[:, :], vecs[0:R, V_LNW + 1:V_LNW + 2],
                                           vecs[0:R, V_LNB + 1:V_LNB + 2], ALU.mult, ALU.add)\
                            .then_inc(S["norm_ready"], 1)
                run_project(pool, step)
                barrier(pool, b, 0)

                def residue(g):
                    pool.wait_ge(S["res_ready"], g * 2 + 2)
                    pool.wait_ge(S["soft_ready"], g * 3 + 3)
                    pool.tensor_tensor(zl[:, :, :], zl[:, :, :], ze[:, :, :], ALU.add).then_inc(S["sp_ready"], 1)

                def times_u(k, c, g):
                    pool.wait_ge(S["dt_ready"], g + 2)
                    pool.wait_ge(S["dbu_ready"], g * NP + 3)
                    for r in range(2):
                        m = pool.tensor_tensor(flat(du[:, r, :]), flat(dt[:, r, :]), chunk(u[:, r], c, k % 2), ALU.mult)
                        m.then_inc(S["du_ready"], 1)
                    pool.wait_ge(S["du_ready"], g * 2 + 2)

                def drive(q, s):
                    pool.wait_ge(S["bs_ready"], s + 2)
                    pool.wait_ge(S["hc_ready"], s + 1)
                    r = 0 if 2 * q < NS else 1
                    pool.tensor_tensor(dbu[:, q, :, :], bs[:, q, :, :],
                                       du[:, r:r + 1, :].to_broadcast([P, 2, T]), ALU.mult).then_inc(S["dbu_ready"], 1)

                def body(k, par, g, before, nxt, after):
                    for q in range(NP):
                        s = g * NP + q
                        if q == 0 or nxt:
                            drive((q + 2) % NP, s + 2)
                        if q == 0 and nxt:
                            times_u(*nxt, g + 1)
                        if q == 2 and after:
                            residue(g + 2)
                g_0 = b * G
                residue(g_0)
                times_u(0, 0, g_0)
                drive(0, g_0 * NP)
                residue(g_0 + 1)
                drive(1, g_0 * NP + 1)
                run_chunks(pool, b, body)
                barrier(pool, b, 1)

                for n, (t, v) in enumerate(((phh[O:O + 1, :], 1.0), (phl[O:O + 1, :], 0.0), (gth[:, :, O:O + 1], 1.0),
                                            (gtl[:, :, O:O + 1], 0.0))):
                    pool.memset(t.bitcast(F32), v).then_inc(S["att_set"], 1)
                    pool.wait_ge(S["att_set"], b * 4 + (n + 1))
                    pool.sem_inc(mark, 1)
                barrier(pool, b, 2)
                barrier(pool, b, 3)

        @block.vector
        def _(dve):
            TT, TS, STT = dve.tensor_tensor, dve.tensor_scalar, dve.scalar_tensor_tensor
            dve.wait_ge(s_load, NL)
            TS(negA[:, :], vecs[:, V_A:V_A + K * NT], ALOG_MAX, None, ALU.min).then_inc(S["consts_set"], 1)
            for r in range(2):
                dve.tensor_reduce(dsum[:, r:r + 1], vecs[:, V_DS + 4 * r:V_DS + 4 * r + 4], AX.X, ALU.add)
            dve.wait_ge(S["consts_set"], 2)
            TS(negA[:, :], negA[:, :], -1.0, None, ALU.mult)
            for name, n in (("x_free", 2), ("fin_ready", 2), ("gated_ready", 2), ("norm_ready", 2), ("gate_ready", 1), ("tap_ready", 2), ("u_ready", 1),
                            ("xlo_ready", 1), ("dt_ready", 1), ("hc_ready", 3), ("cbc_ready", 4), ("summed", 4), ("y_added", 1),
                            ("bs_ready", 1), ("dbu_ready", 3), ("dtpre_ready", 1), ("phl_ready", 1), ("gtl_ready", 1),
                            ("top_read", 2), ("pf_ready", 2), ("yraw_ready", 1), ("pv_ready", 2), ("pl_ready", 2),
                            ("yn_ready", 1), ("out_stored", 32)):
                dve.sem_inc(S[name], n)
            barrier(dve, 0, -1)

            def link(ins, name, n):
                ins.then_inc(S[name], 1)
                dve.wait_ge(S[name], n)

            with dve.Fori(0, nb) as b:
                def deviate(n, srca, srcb):
                    dve.wait_ge(S["mean_ready"], n + 1)
                    TT(da[:, :], srca, ps[:, 0, :], ALU.subtract).then_inc(S["dev_ready"], 1)
                    TT(db[:, :], srcb, ps[0:R, 0, :], ALU.subtract).then_inc(S["dev_ready"], 1)

                FIRST_TAPS = 7
                def convolve(c, part):
                    w = b * NCH + c
                    for n in (range(FIRST_TAPS), range(FIRST_TAPS, 8))[part]:
                        t = n if n < 4 else n + 1
                        dy, dx = t // 3, t % 3
                        for r in range(2):
                            acc = chunk(u[:, r], c, 0)
                            src = padi[r][:, bass.ds(c * RPC + dy, RPC), dx:dx + WW]
                            if n > 0:
                                dve.wait_ge(S["conv_link"], w * 14 + (2 * n - 1 + r))
                            STT(acc, src, vecs[:, V_TAP + 9 * r + t:V_TAP + 9 * r + t + 1], acc, ALU.mult, ALU.add)\
                                .then_inc(S["conv_link" if n < 7 else "conv_ready"], 1)

                def step(c, par, which):
                    i, j = b * NCH + c, b * NCH + (c + 1)
                    n = (b * 2) * NCH + (c + 1)
                    q = 1 - par
                    if "n" in which:
                        dve.wait_ge(S["norm_ready"], j * 2 + 2)
                        deviate(n, xa[:, q, :], xb[:, q, :])
                        dve.wait_ge(S["dev_ready"], n * 2 + 2)
                        dve.sem_inc(S["x_free"], 1)
                    if "c" in which:
                        dve.wait_ge(S["borders_set"], b * 8 + 8)
                        if isinstance(c, int) and c > NCH:
                            dve.wait_ge(S["tap_ready"], (b * NCH + (c - 2)) * 2 + 4)
                        else:
                            dve.wait_ge(S["tap_ready"], (b * NCH + (c - 1)) * 2 + 4)
                        convolve(c - 2, 0)
                    if "n" in which:
                        dve.wait_ge(S["rstd_ready"], n * 2 + 2)
                        TT(da[:, :], da[:, :], rstd[:, :], ALU.mult).then_inc(S["scaled"], 1)
                        TT(db[:, :], db[:, :], rstd[0:R, :], ALU.mult).then_inc(S["scaled"], 1)
                    if "p" in which:
                        dve.wait_ge(S["zs_ready"], i * 3 + 3)
                        TT(gate[:, :, bass.ds(c * T, T)], ps[:, 4:6, :], zs[:, :, :], ALU.mult)\
                            .then_inc(S["gate_ready"], 1)
                    if "c" in which:
                        convolve(c - 2, 1)
                run_project(dve, step)
                barrier(dve, b, 0)

                dve.memset(xd[:, :], 1.0).then_inc(S["zero_h"], 1)
                dve.memset(h[:, :, T - 1:T], 0.0).then_inc(S["zero_h"], 1)
                dve.wait_ge(S["zero_h"], b * (K + 1) + 2)
                dve.sem_inc(S["scan_set"], 1)

                def low_half(par, g):
                    dve.wait_ge(S["xhi_ready"], g + 1)
                    TT(xhl[par][LO:LO + 32, :], ps[LO:LO + 32, 0, :], xhl[par][LO:LO + 32, :].bitcast(F32),
                       ALU.subtract).then_inc(S["xlo_ready"], 1)

                def residue(g):
                    dve.wait_ge(S["soft_ready"], g * 3 + 2)
                    TS(ze[:, :, :], za[:, :, :], 1.0, -1.0, ALU.add, ALU.add).then_inc(S["res_ready"], 1)
                    dve.wait_ge(S["res_ready"], g * 2 + 1)
                    TT(ze[:, :, :], za[:, :, :], ze[:, :, :], ALU.subtract).then_inc(S["res_ready"], 1)

                def softplus(g):
                    dve.wait_ge(S["sp_ready"], g + 1)
                    STT(dt[:, :, :], ps[:, 6:8, :], 0.0, zl[:, :, :], ALU.max, ALU.add).then_inc(S["dt_ready"], 1)

                def scans(k, q, s):
                    step = -1 if k >= 2 else 1
                    end = T - 1 if step == 1 else 0
                    dve.wait_ge(S["dA_ready"], s * 2 + 2)
                    dve.wait_ge(S["dbu_ready"], s + 4)
                    for e in range(2):
                        j = 2 * q + e
                        dve.tensor_tensor_scan(h[:, j, ::step], dA[:, q, e, ::step], dbu[:, q, e, ::step],
                                               h[:, j, end:end + 1], ALU.mult, ALU.add)\
                            .then_inc(S["scan_link"], 1)

                def times_c(q, s):
                    dve.wait_ge(S["scan_link"], s * 2 + 2)
                    dve.wait_ge(S["cbc_ready"], s + 5)
                    dve.wait_ge(S["summed"], s + 2)
                    TT(hc[:, q, :, :], h[:, 2 * q:2 * q + 2, :], ps[:, 4:6, :], ALU.mult).then_inc(S["hc_ready"], 1)

                def add_y(k, c, g):
                    dve.wait_ge(S["summed"], g * NP + (NP + 4))
                    if isinstance(c, int) or k >= 2:
                        dve.sem_inc(mark, 1)
                    for r, (lo, bank) in enumerate(((0, 1), (R, 0))):
                        y = chunk(Y[r], c, k % 2, lo, P)
                        if k == 0:
                            ins = STT(y, chunk(u[:, r], c, 0, lo, P), dsum[lo:P, r:r + 1], flat(ps[lo:P, bank, :]),
                                      ALU.mult, ALU.add)
                        else:
                            ins = TT(y, flat(ps[lo:P, bank, :]), y, ALU.add)
                    ins.then_inc(S["y_added"], 1)

                def body(k, par, g, before, nxt, after):
                    for q in range(NP):
                        s = g * NP + q
                        scans(k, q, s)
                        if q == 0 and nxt:
                            low_half(1 - par, g + 1)
                        times_c(q, s)
                        if q == 0 and nxt:
                            dve.wait_ge(S["dA_ready"], g * NT + NT)
                            dve.wait_ge(S["du_ready"], g * 2 + 2)
                            softplus(g + 1)
                        if q == 1 and before:
                            add_y(*before, g - 1)
                        if q == 2 and after:
                            residue(g + 2)
                    if nxt and nxt[0] != k:
                        end = T - 1 if nxt[0] < 2 else 0
                        dve.wait_ge(S["hc_ready"], g * NP + (NP + 3))
                        dve.sem_inc(mark, 1)
                        dve.memset(h[:, :, end:end + 1], 0.0).then_inc(S["zero_h"], 1)
                        dve.wait_ge(S["zero_h"], b * (K + 1) + (k + 3))
                        dve.sem_inc(mark, 1)
                g_0 = b * G
                low_half(0, g_0)
                residue(g_0)
                softplus(g_0)
                residue(g_0 + 1)
                run_chunks(dve, b, body)
                add_y(K - 1, 0, g_0 + G - 1)
                barrier(dve, b, 1)

                i_0 = b * NCH
                dve.memset(mx[:, :, 0:1], -3.0e38).then_inc(S["mx_link"], 1)

                def low_theta(i, par):
                    dve.wait_ge(S["thh_ready"], i + 1)
                    TT(thc[par][1][0:O, :], thf[:, :], thc[par][0][0:O, :].bitcast(F32), ALU.subtract)\
                        .then_inc(S["thl_ready"], 1)

                def early_top(m, t, col, bank):
                    dve.wait_ge(S["top_ready"], i_0 * NU + m * 4 + (t + 1))
                    dve.tensor_reduce(mx[:, t, col:col + 1], ps[:, bank, :], AX.X, ALU.max).then_inc(S["top_read"], 1)

                def step(c, par, which):
                    i, j = b * NCH + c, b * NCH + (c + 1)
                    n = (b * 2 + 1) * NCH + (c + 1)
                    if "n" in which:
                        dve.wait_ge(S["gated_ready"], j * 2 + 2)
                        deviate(n, pad0[:, bass.ds((c + 1) * T, T)], yt[:, 1 - par, :])
                    if "p" in which:
                        dve.wait_ge(S["mixed"], i + 1)
                        dve.wait_ge(S[f"x_loaded{par}"], (b * 2 + 1) * (16 * NCH) + (c - par) * 16 + 32)
                        dve.wait_ge(S["gtl_ready"], i + 1)
                        TT(na[:, :], ps[:, 2, :], xa[:, par, :], ALU.add).then_inc(S["x1_ready"], 1)
                        TT(nb_[:, :], ps[0:R, 3, :], xb[:, par, :], ALU.add).then_inc(S["x1_ready"], 1)
                        dve.wait_ge(S["x1_ready"], i * 2 + 2)
                        dve.sem_inc(S["x_free"], 1)
                        early = not (isinstance(c, int) and c == 0)
                        if early:
                            early_top(c - 1, 0, 1 + par, 6)
                            early_top(c - 1, 1, 1 + par, 7)
                    if "n" in which:
                        dve.wait_ge(S["rstd_ready"], n * 2 + 2)
                        at = j * 4
                        link(TT(da[:, :], da[:, :], rstd[:, :], ALU.mult), "mix_link", at + 1)
                        link(TT(db[:, :], db[:, :], rstd[0:R, :], ALU.mult), "mix_link", at + 2)
                        link(TS(da[:, :], da[:, :], vecs[:, V_ONW:V_ONW + 1], vecs[:, V_ONB:V_ONB + 1],
                                ALU.mult, ALU.add), "mix_link", at + 3)
                        link(TS(db[:, :], db[:, :], vecs[0:R, V_ONW + 1:V_ONW + 2], vecs[0:R, V_ONB + 1:V_ONB + 2],
                                ALU.mult, ALU.add), "mix_link", at + 4)
                        sl = bass.ds((c + 1) * T, T)
                        TT(oa[:, :], da[:, :], gate[:, 0, sl], ALU.mult).then_inc(S["gated_ready"], 1)
                        TT(ob[:, :], db[:, :], gate[0:R, 1, sl], ALU.mult).then_inc(S["gated_ready"], 1)
                    if "p" in which:
                        sl = bass.ds(c * T, T)
                        dve.wait_ge(S["phh_ready"], i + 1)
                        TT(phl[0:O, sl], phf[:, :], phh[0:O, sl].bitcast(F32), ALU.subtract)\
                            .then_inc(S["phl_ready"], 1)
                        dve.wait_ge(S["gth_ready"], i + 1)
                        gs = bass.ds(c * 4, 4)
                        TT(gtl[:, gs, 0:O], ps[:, 5, :].rearrange("p (t n) -> p t n", n=P)[:, :, 0:O],
                           gth[:, gs, 0:O].bitcast(F32), ALU.subtract).then_inc(S["gtl_ready"], 1)
                        if early:
                            early_top(c - 1, 2, 1 + par, 6)
                            early_top(c - 1, 3, 1 + par, 7)
                            dve.wait_ge(S["top_read"], i_0 * NU + c * 4 + 2)
                            dve.wait_ge(S["mx_link"], i_0 + c)
                            TT(mx[:, :, 0:1], mx[:, :, 0:1], mx[:, :, 1 + par:2 + par], ALU.max)\
                                .then_inc(S["mx_link"], 1)
                        else:
                            low_theta(i, 0)
                run_mix(dve, step)
                barrier(dve, b, 2)

                def top(j, i):
                    dve.wait_ge(S["top_ready"], i * NU + (j + 1))
                    t, m = j // (NU // 4), j % (NU // 4)
                    dve.tensor_reduce(mx[:, t, m:m + 1], ps[:, 5 + j % 2, :], AX.X, ALU.max)\
                        .then_inc(S["top_read"], 1)

                def negate(i, first=False):
                    dve.wait_ge(S["top_read"], i * NU + NU + 2)
                    if first:
                        dve.wait_ge(S["mx_link"], i + NCH)
                        dve.tensor_reduce(nmx[:, :], mx[:, :, 0:4], AX.X, ALU.max, negate=True)\
                            .then_inc(S["nmx_ready"], 1)
                    else:
                        dve.wait_ge(S["shift_ready"], i)
                        dve.tensor_reduce(nmx[:, :], mx[:, :, :], AX.X, ALU.max, negate=True)\
                            .then_inc(S["nmx_ready"], 1)

                def low_exp(mp, s):
                    dve.wait_ge(S["ph_ready"], s + 1)
                    TT(pl[:, mp % 2, :, :], pf[:, mp % 2, :, :], ph[:, mp % 2, :, :].bitcast(F32), ALU.subtract)\
                        .then_inc(S["pl_ready"], 1)

                def invert(i):
                    dve.wait_ge(S["den_ready"], i + 1)
                    dve.reciprocal(rcol[:, :], ps[:, 7, 0:4]).then_inc(S["inv_link"], 1)
                    dve.wait_ge(S["inv_link"], i + 1)
                    for t in range(4):
                        m = TS(rbt[:, t, :], ones[:, 0:O], rcol[:, t:t + 1], None, ALU.mult)
                    m.then_inc(S["rden_ready"], 1)

                def divide(i):
                    dve.wait_ge(S["rb_ready"], i + 1)
                    TT(yn[:, :], yraw[0:O, :], ps[0:O, 7, :], ALU.mult).then_inc(S["yn_ready"], 1)

                def finish(c, i, part):
                    dve.wait_ge(S["wy_ready"], i * 2 + (part + 1))
                    if part == 0:
                        dve.wait_ge(S["out_stored"], i * 32 + 32)
                    hi = (P, R)[part]
                    STT(fa[0:hi, part, :], ps[0:hi, 7, :], vecs[0:hi, V_WB + part:V_WB + part + 1],
                        (pad0, pad1)[part][0:hi, bass.ds(c * T, T)], ALU.add, ALU.add).then_inc(S["fin_ready"], 1)

                i_0 = b * NCH

                def attend(c, par, before, nxt):
                    i = i_0 + c
                    for mp in range(MP):
                        if mp == 1 and nxt:
                            low_theta(i + 1, 1 - par)
                        if nxt:
                            for j in range(FIRST_TOP[mp], FIRST_TOP[mp] + TOPS[mp]):
                                top(j, i + 1)
                            if mp > 0 and FIRST_TOP[mp] == NU and FIRST_TOP[mp - 1] < NU:
                                negate(i + 1)
                        low_exp(mp, i * MP + mp)
                        if before:
                            if mp == DEN_AT:
                                invert(i - 1)
                            if mp == RB_AT:
                                divide(i - 1)
                            if mp == WY_AT:
                                finish(c - 1, i - 1, 0)
                            if mp == WR_AT:
                                finish(c - 1, i - 1, 1)
                for q in range(2):
                    dve.memset(thc[q][1][O:O + 1, :].bitcast(F32), 0.0).then_inc(S["thc_set"], 1)
                for t in range(4):
                    early_top(NCH - 1, t, 3, 5 + t % 2)
                negate(i_0, True)
                run_attend(dve, attend)
                last = i_0 + (NCH - 1)
                invert(last)
                divide(last)
                finish(NCH - 1, last, 0)
                finish(NCH - 1, last, 1)
                barrier(dve, b, 3)


def kernel(x, L0_conv_ln_w, L0_conv_ln_b, L0_conv_in_proj_w, L0_conv_conv_w, L0_conv_conv_b, L0_conv_x_proj_w,
           L0_conv_dt_proj_w, L0_conv_dt_proj_b, L0_conv_A_log, L0_conv_Ds, L0_conv_out_norm_w, L0_conv_out_norm_b,
           L0_conv_out_proj_w, L1_conv_g_w, L1_conv_g_b, L1_conv_theta_w, L1_conv_theta_b, L1_conv_phi_w,
           L1_conv_phi_b, L1_conv_W_w, L1_conv_W_b, _nb=B, _run=None):
    f = lambda a: np.ascontiguousarray(np.asarray(a))
    rem2 = lambda a: np.concatenate([a[..., P:C], a[..., P:C]], -1)

    vec = np.zeros((P, NV), np.float32)

    def put(col, v, twice=False):
        v = f(v)
        vec[:, col] = v[:P]
        vec[:, col + 1] = rem2(v)
    for col, v in ((V_LNW, L0_conv_ln_w), (V_LNB, L0_conv_ln_b), (V_CB, L0_conv_conv_b), (V_ONW, L0_conv_out_norm_w),
                   (V_ONB, L0_conv_out_norm_b), (V_WB, L1_conv_W_b)):
        put(col, v)
    ds, al, cw = f(L0_conv_Ds), f(L0_conv_A_log), f(L0_conv_conv_w).reshape(C, 9)
    for k in range(K):
        vec[:, V_DS + k], vec[:, V_DS + 4 + k] = ds[k, :P], rem2(ds[k])
        for n in range(NS):
            vec[:, V_A + k * NT + n] = al[k, :P, n]
        for m in range(NS // 2):
            vec[:, V_A + k * NT + NS + m] = np.concatenate([al[k, P:, 2 * m], al[k, P:, 2 * m + 1]])
    for t in range(9):
        vec[:, V_TAP + t], vec[:, V_TAP + 9 + t] = cw[:P, t], rem2(cw[:, t])
    vec[:O, V_TB], vec[:O, V_PB] = f(L1_conv_theta_b), f(L1_conv_phi_b)

    wi = f(L0_conv_in_proj_w).T
    w_in = np.concatenate([wi[:, :P], rem2(wi[:, :C]), wi[:, C:C + P], rem2(wi[:, C:])], 1)
    xp, dp, db = f(L0_conv_x_proj_w), f(L0_conv_dt_proj_w), f(L0_conv_dt_proj_b)
    w_x = np.zeros((2 * P, K * 64), np.float32)
    w_dt = np.zeros((NX + 1, K * 2 * P), np.float32)
    for k in range(K):
        w_x[:C, 64 * k:64 * k + NX] = w_x[:C, 64 * k + LO:64 * k + LO + NX] = xp[k].T
        both = np.concatenate([dp[k].T, np.zeros((2 * NS, C), np.float32), db[k][None]], 0)
        w_dt[:, 2 * k * P:(2 * k + 1) * P], w_dt[:, (2 * k + 1) * P:(2 * k + 2) * P] = both[:, :P], rem2(both)
    sel = np.zeros((64, 2 * NT, P), np.float32)
    for w in range(2):
        for j in range(NT):
            for p in range(P):
                n = j if j < NS else 2 * (j - NS) + p // R
                sel[RANK + w * NS + n, w * NT + j, p] = sel[LO + RANK + w * NS + n, w * NT + j, p] = 1.0
    arrays = {
        "x": f(x)[:_nb], "vec": vec, "w_in": w_in, "w_x": w_x, "w_dt": w_dt, "sel": sel.reshape(64, 2 * NT * P),
        "fold": np.concatenate([np.eye(R, dtype=np.float32)] * 2, 0), "ident": np.eye(P, dtype=np.float32),
        "w_out": f(L0_conv_out_proj_w).T,
        "w_att": np.concatenate([f(L1_conv_theta_w).T, f(L1_conv_phi_w).T, f(L1_conv_g_w).T], 1),
        "gb": f(L1_conv_g_b)[None], "w_w": f(L1_conv_W_w).T,
    }
    arrays = {f"in_{n}": np.ascontiguousarray(a) for n, a in arrays.items()}
    import concourse.bacc as bacc
    from concourse.bass_utils import run_bass_kernel_spmd
    nc = bacc.Bacc("TRN2", target_bir_lowering=False, num_devices=1)
    aps = [nc.dram_tensor(n, a.shape, F32, kind="ExternalInput").ap() for n, a in arrays.items()]
    res = nc.dram_tensor("out", [_nb, C, HH, WW], F32, kind="ExternalOutput").ap()
    build(nc, _nb, *aps, res)
    if _run:
        return _run(nc, arrays)
    return run_bass_kernel_spmd(nc, [arrays], core_ids=[0]).results[0]["out"]
```
